# Optimizing a Trainium2 kernel written in Bass

```python
import numpy as np
import jax
import jax.numpy as jnp

def _softmax(x, axis=-1):
    return jax.nn.softmax(x, axis=axis)

def _gelu(x):
    return jax.nn.gelu(x, approximate=True)

def _silu(x):
    return jax.nn.silu(x)

def _sigmoid(x):
    return jax.nn.sigmoid(x)

def _layernorm(x, axis=-1, eps=1e-05):
    m = jnp.mean(x, axis=axis, keepdims=True)
    v = jnp.var(x, axis=axis, keepdims=True)
    return (x - m) / jnp.sqrt(v + eps)

def _scatter_add(tgt, idx, src, axis=0):
    return tgt.at[idx].add(src)

def _segment_sum(src, seg, n):
    return jax.ops.segment_sum(src, seg, n)
kernel_name = 'mk_decoder_preln_d1_seqx_r8_c12b9b'

def setup_inputs(seed: int=0):
    np.random.seed(seed)
    _w = jnp.asarray

    def _rec_inputs():
        import jax
        import jax.numpy as jnp
        _rk = jax.random.key(seed)
        x = -0.000125 + 0.9999 * jax.random.normal(jax.random.fold_in(_rk, 1), (4, 256, 256), jnp.float32)
        _lenS = 256 - jax.random.randint(jax.random.fold_in(_rk, 7), (4,), 0, max(1, 256 // 4) + 1, jnp.int32)
        _lenS2 = 256 - jax.random.randint(jax.random.fold_in(_rk, 8), (4,), 0, max(1, 256 // 4) + 1, jnp.int32)
        itok_BxS_13_99985 = jax.random.randint(jax.random.fold_in(_rk, 11), (4, 256), 13, 99986, jnp.int32)
        _ctx_2048P = jax.random.normal(jax.random.fold_in(_rk, 12), (4, 16, 256), jnp.float32)
        _ctx_2048c = jax.random.dirichlet(jax.random.fold_in(_rk, 512), 0.3 * jnp.ones((16,), jnp.float32), (4, 256))
        _ctx_2048t = jnp.einsum('bsk,bkd->bsd', _ctx_2048c, _ctx_2048P)
        _ctx_2048t = _ctx_2048t * jax.lax.rsqrt(jnp.mean(jnp.square(_ctx_2048t)) + 1e-12) * 0.953939
        ctx_2048 = 6.82029e-06 + 0.0200006 * (_ctx_2048t + 0.3 * jax.random.normal(jax.random.fold_in(_rk, 612), (4, 256, 256), jnp.float32))
        return (x, itok_BxS_13_99985, ctx_2048)
    x, itok_BxS_13_99985, ctx_2048 = _rec_inputs()

    def _L0_attn_setup():
        import math
        import jax, jax.numpy as jnp
        import numpy as np
        NUM_HEAD = 16
        EMB = 256
        HEAD_DIM = EMB // NUM_HEAD
        B, T = (2, 256)

        def get_slopes(n):
            start = 2 ** (-2 ** (-(math.log2(n) - 3)))
            return np.array([start * start ** i for i in range(n)], dtype=np.float32)
        key = jax.random.key(seed)
        ks = jax.random.split(key, 5)
        x = jax.random.normal(ks[0], (B, T, EMB), jnp.float32)

        def w(k, scale=0.02):
            return jax.random.normal(k, (EMB, EMB), jnp.float32) * scale
        return {'x': x, 'Wq': w(ks[1]), 'bq': jnp.zeros((EMB,), jnp.float32), 'Wk': w(ks[2]), 'bk': jnp.zeros((EMB,), jnp.float32), 'Wv': w(ks[3]), 'bv': jnp.zeros((EMB,), jnp.float32), 'Wo': w(ks[4], scale=0.02 / math.sqrt(24)), 'bo': jnp.zeros((EMB,), jnp.float32)}
    _L0_attn_all = _L0_attn_setup()
    _L0_attn_in = {k: v for k, v in _L0_attn_all.items() if k in ('Wq', 'bq', 'Wk', 'bk', 'Wv', 'bv', 'Wo', 'bo')}
    del _L0_attn_all

    def _L0_xattn_setup():
        import jax, jax.numpy as jnp
        import numpy as np
        B, S, D = (4, 512, 256)
        E = 4
        F = 1024 // E
        VOCAB = 12500
        key = jax.random.key(seed)
        k1, k2, k3, k4, k5 = jax.random.split(key, 5)
        hidden_states = jax.random.normal(k1, (B, S, D), dtype=jnp.float32)
        token_ids = jax.random.randint(k2, (B, S), 0, VOCAB, dtype=jnp.int64)
        Wg = jax.random.normal(k3, (E, F, D), dtype=jnp.float32) * 0.02
        Wu = jax.random.normal(k4, (E, F, D), dtype=jnp.float32) * 0.02
        Wd = jax.random.normal(k5, (E, D, F), dtype=jnp.float32) * 0.02
        return {'hidden_states': hidden_states, 'token_ids': token_ids, 'Wg': Wg, 'Wu': Wu, 'Wd': Wd}
    _L0_xattn_all = _L0_xattn_setup()
    _L0_xattn_in = {k: v for k, v in _L0_xattn_all.items() if k in ()}
    del _L0_xattn_all

    def _L0_ffn_setup():
        import jax, jax.numpy as jnp
        import numpy as np
        NUM_EXPERTS = 64
        TOP_K = 8
        HIDDEN = 256
        INTER = 128
        key = jax.random.key(seed)
        k1, k2, k3, k4 = jax.random.split(key, 4)
        scale = 1.0 / np.sqrt(HIDDEN)
        hidden_states = jax.random.normal(k1, (4, 256, HIDDEN), dtype=jnp.float32)
        gate_w = jax.random.normal(k2, (NUM_EXPERTS, HIDDEN), dtype=jnp.float32) * scale
        w13 = jax.random.normal(k3, (NUM_EXPERTS, 2 * INTER, HIDDEN), dtype=jnp.float32) * scale
        w2 = jax.random.normal(k4, (NUM_EXPERTS, HIDDEN, INTER), dtype=jnp.float32) * (1.0 / np.sqrt(INTER))
        return {'hidden_states': hidden_states, 'gate_w': gate_w, 'w13': w13, 'w2': w2}
    _L0_ffn_all = _L0_ffn_setup()
    _L0_ffn_in = {k: v for k, v in _L0_ffn_all.items() if k in ('gate_w', 'w13', 'w2')}
    del _L0_ffn_all
    return {'x': x, 'itok_BxS_13_99985': itok_BxS_13_99985, 'ctx_2048': ctx_2048, 'L0_attn_Wq': _L0_attn_in['Wq'], 'L0_attn_bq': _L0_attn_in['bq'], 'L0_attn_Wk': _L0_attn_in['Wk'], 'L0_attn_bk': _L0_attn_in['bk'], 'L0_attn_Wv': _L0_attn_in['Wv'], 'L0_attn_bv': _L0_attn_in['bv'], 'L0_attn_Wo': _L0_attn_in['Wo'], 'L0_attn_bo': _L0_attn_in['bo'], 'L0_ffn_gate_w': _L0_ffn_in['gate_w'], 'L0_ffn_w13': _L0_ffn_in['w13'], 'L0_ffn_w2': _L0_ffn_in['w2']}

def reference(x, itok_BxS_13_99985, ctx_2048, L0_attn_Wq, L0_attn_bq, L0_attn_Wk, L0_attn_bk, L0_attn_Wv, L0_attn_bv, L0_attn_Wo, L0_attn_bo, L0_ffn_gate_w, L0_ffn_w13, L0_ffn_w2):
    import jax
    import jax.numpy as jnp

    def _L0_attn_ref(x, Wq, bq, Wk, bk, Wv, bv, Wo, bo):
        import math
        import jax, jax.numpy as jnp
        import numpy as np
        NUM_HEAD = 16
        EMB = 256
        HEAD_DIM = EMB // NUM_HEAD
        B, T = (2, 256)

        def get_slopes(n):
            start = 2 ** (-2 ** (-(math.log2(n) - 3)))
            return np.array([start * start ** i for i in range(n)], dtype=np.float32)
        Bx, Tx, C = x.shape
        slopes = jnp.asarray(get_slopes(NUM_HEAD))

        def split_heads(y):
            return y.reshape(Bx, Tx, NUM_HEAD, HEAD_DIM).transpose(0, 2, 1, 3)
        q = split_heads(x @ Wq + bq)
        k = split_heads(x @ Wk + bk)
        v = split_heads(x @ Wv + bv)
        attn = jnp.einsum('bhqd,bhkd->bhqk', q, k) / jnp.sqrt(jnp.float32(HEAD_DIM))
        alibi = -slopes[:, None, None] * (Tx - 1 - jnp.arange(Tx, dtype=jnp.float32))[None, None, :]
        attn = attn + alibi
        causal = jnp.tril(jnp.ones((Tx, Tx), dtype=bool))[None, None]
        attn = jnp.where(causal, attn, jnp.finfo(jnp.float32).min)
        p = jax.nn.softmax(attn, axis=-1)
        out = jnp.einsum('bhqk,bhkd->bhqd', p, v).transpose(0, 2, 1, 3).reshape(Bx, Tx, C)
        return out @ Wo + bo

    def _L0_xattn_ref(hidden_states, token_ids, Wg, Wu, Wd):
        import jax, jax.numpy as jnp
        import numpy as np
        B, S, D = (4, 512, 256)
        E = 4
        F = 1024 // E
        VOCAB = 12500
        tokens_per_expert = VOCAB // E
        tid = jnp.clip(token_ids, 0, VOCAB - 1)
        expert_ids = jnp.minimum(tid // tokens_per_expert, E - 1)
        out = jnp.zeros_like(hidden_states)
        for e in range(E):
            g = jax.nn.silu(jnp.einsum('bsd,fd->bsf', hidden_states, Wg[e]))
            u = jnp.einsum('bsd,fd->bsf', hidden_states, Wu[e])
            y = jnp.einsum('bsf,df->bsd', g * u, Wd[e])
            out = jnp.where((expert_ids == e)[..., None], y, out)
        return out

    def _L0_ffn_ref(hidden_states, gate_w, w13, w2):
        import jax, jax.numpy as jnp
        import numpy as np
        NUM_EXPERTS = 64
        TOP_K = 8
        HIDDEN = 256
        INTER = 128
        orig_shape = hidden_states.shape
        x = hidden_states.reshape(-1, HIDDEN)
        logits = jnp.einsum('th,eh->te', x, gate_w)
        probs = jax.nn.softmax(logits, axis=-1)
        topk_w, topk_idx = jax.lax.top_k(probs, TOP_K)
        combine = (jax.nn.one_hot(topk_idx, NUM_EXPERTS, dtype=x.dtype) * topk_w[..., None]).sum(axis=1)

        def step(acc, inp):
            w13_e, w2_e, c = inp
            g = x @ w13_e[:INTER].T
            u = x @ w13_e[INTER:].T
            h = jax.nn.silu(g) * u
            o = h @ w2_e.T
            return (acc + c[:, None] * o, None)
        out0 = jnp.zeros_like(x)
        out, _ = jax.lax.scan(step, out0, (w13, w2, combine.T))
        return out.reshape(orig_shape)
    x = x + _L0_attn_ref(_layernorm(x, axis=-1), L0_attn_Wq, L0_attn_bq, L0_attn_Wk, L0_attn_bk, L0_attn_Wv, L0_attn_bv, L0_attn_Wo, L0_attn_bo)
    x = x + _L0_xattn_ref(_layernorm(x, axis=-1), itok_BxS_13_99985, ctx_2048, ctx_2048, ctx_2048)
    x = x + _L0_ffn_ref(_layernorm(x, axis=-1), L0_ffn_gate_w, L0_ffn_w13, L0_ffn_w2)
    return x

_drawn_inputs = setup_inputs


def setup_inputs(seed=0):
    import zlib

    import numpy as np

    out = dict(_drawn_inputs(seed))
    spreads = {'L0_attn_bq': (0.0, 0.8),
     'L0_attn_bk': (0.0, 0.8),
     'L0_attn_bv': (0.0, 0.8),
     'L0_attn_bo': (0.0, 0.1)}
    factors = {'L0_attn_Wq': 8.0, 'L0_attn_Wk': 8.0, 'L0_attn_Wv': 7.332, 'L0_attn_Wo': 5.409}
    for name, (base, spread) in spreads.items():
        noise = np.random.default_rng([zlib.crc32(name.encode()), seed]).standard_normal(out[name].shape)
        drawn = base * np.exp(spread * noise) if base else spread * noise
        out[name] = jnp.asarray(drawn.astype(out[name].dtype))
    for name, factor in factors.items():
        out[name] = (out[name] * factor).astype(out[name].dtype)
    return out
```

```python
from contextlib import ExitStack

import concourse.bass as bass
from concourse import mybir

ALU = mybir.AluOpType
ACT = mybir.ActivationFunctionType
F32 = mybir.dt.float32
BF16 = mybir.dt.bfloat16
I32 = mybir.dt.int32
U32 = mybir.dt.uint32
AX_X = mybir.AxisListType.X

P = 128
B, S, D = 4, 256, 256
TOK = B * S
NT = TOK // P
TB = S // P
KD = D // P
H, HD = 16, 16
SLOT = 32
GH = P // SLOT
NG = H // GH
HV = HD + 1
SC = P + S
EX, CTX = 4, 256
THIRD = 12500 // EX
E, TOPK, F = 64, 8, 128
CAP = TOK
COLS = E * CAP // P
NQ = COLS // P
CHAINS = 4
MAXT = 128
EMPTY = 4096
EPS = 1e-5
C_ID, C_TRI, C_IOTA, C_PQ, C_SLOT, C_TOK, C_E8 = 0, 128, 256, 384, 388, 452, 460
C_W = 461


def decoder_kernel(nc, x, tok_ids, ctx_t, wqk, wv, wo, bqk, rows, gate_t, w13_t, w2_t, consts, neg_bias, out):
    with ExitStack() as ctx:
        def sb(name, shape, dt=F32):
            return ctx.enter_context(nc.sbuf_tensor(name, shape, dt))

        def sem(name):
            return ctx.enter_context(nc.semaphore(name))

        rows_dram = nc.dram_tensor("rows_dram", (TOK, D), F32).ap()
        table_dram = [nc.dram_tensor(f"table_dram{i}", (E * CAP, 2), F32).ap() for i in range(CHAINS)]
        sums_dram = [nc.dram_tensor(f"sums_dram{i}", (TOK, D), F32).ap() for i in range(CHAINS)]

        X = sb("X", [P, NT, D])
        XB = sb("XB", [P, NT, D])
        TID = sb("TID", [P, NT], I32)
        CT = sb("CT", [P, KD, EX * CTX])
        WQK = sb("WQK", [P, KD, 2, NG * P])
        WV = sb("WV", [P, KD, D])
        WO = sb("WO", [P, KD, D])
        BQK = sb("BQK", [P, 2, NG])
        BQN = sb("BQN", [P, NG])
        BROW = sb("BROW", [P, 2, D])
        GT = sb("GT", [P, KD, E])
        C = sb("C", [P, C_W])
        NB = sb("NB", [P, H, SC])
        ZERO = sb("ZERO", [P, 2048])
        NEGH = sb("NEGH", [P, TB])
        TRI = sb("TRI", [P, P], BF16)
        ONES = sb("ONES", [P, P], BF16)
        ONEF = sb("ONEF", [P, P])
        GE = sb("GE", [P, 3, NT])
        MSK = sb("MSK", [P, NT, EX])

        ST = sb("ST", [P, TB, 6])
        MV = sb("MV", [P, TB, 2])
        VE = sb("VE", [P, TB])
        RSTD = sb("RSTD", [P, TB])
        XN = sb("XN", [P, TB, D])
        XT = sb("XT", [P, KD, S])
        QT = sb("QT", [P, NG, S])
        KT = sb("KT", [P, NG, S])
        VA = sb("VA", [P, TB, H, HV])
        MN = sb("MN", [P, H, 2])
        PR = sb("PR", [P, 2, SC])
        PT = sb("PT", [P, 2, SC])
        RS = sb("RS", [P, TB, H])
        AO = sb("AO", [P, TB, H, HD])
        X2 = sb("X2", [P, TB, D])
        Z = sb("Z", [P, TB, CTX])
        TH = sb("TH", [P, TB, CTX])
        AA = sb("AA", [P, TB, CTX])
        X3 = sb("X3", [P, NT, D])
        ML = sb("ML", [P, TB, 8])
        NM = sb("NM", [P, TB])
        EL = sb("EL", [P, TB, E])
        SE = sb("SE", [P, TB])
        RE = sb("RE", [P, TB])
        PB = sb("PB", [P, TB, E])
        M8 = sb("M8", [P, TB, 8])
        PX = sb("PX", [P, TB, E])
        SEL = sb("SEL", [P, TB, E])
        SELB = sb("SELB", [P, TB, E], BF16)
        CNT = sb("CNT", [P, E], BF16)
        CW = sb("CW", [P, TB, E])
        SV = sb("SV", [P, TB, E])
        V8 = sb("V8", [P, TB, 8])
        IX = sb("IX", [P, TB, 8], I32)
        EQ = sb("EQ", [P, TB, 8, E])
        DT = sb("DT", [P, TB, 8, 2])

        TABLE = sb("TABLE", [P, CHAINS, NQ, P * 2])
        NI = sb("NI", [E, 4], I32)
        NBF = sb("NBF", [E, 1], BF16)
        SN = sb("SN", [E, 4])
        M1 = sb("M1", [E, P])
        M2 = sb("M2", [E, P])
        CB = sb("CB", [P, P])
        LATE = sb("LATE", [P, P])
        NTF = sb("NTF", [P, 1])
        OH = sb("OH", [P, NQ, P])
        IW = sb("IW", [P, MAXT + CHAINS, 2])
        EJ = sb("EJ", [1, 3, MAXT], I32)
        NQI = sb("NQI", [1, 4], I32)

        XR = sb("XR", [P, CHAINS, D])
        IG = sb("IG", [P, CHAINS], I32)
        IS = sb("IS", [P, CHAINS], I32)
        XRT = sb("XRT", [P, CHAINS, KD, P])
        W13 = sb("W13", [P, CHAINS, KD, 2 * F])
        W2 = sb("W2", [P, CHAINS, D])
        SG = sb("SG", [P, CHAINS, P])
        HT = sb("HT", [P, CHAINS, P])
        OB = sb("OB", [P, CHAINS, D])

        ps = ctx.enter_context(nc.psum_tensor("ps", [P, 8, 512], F32))

        ident = C[:, C_ID:C_ID + P]
        iota = C[:, C_IOTA:C_IOTA + P]
        nb_flat = NB[:, :, :].rearrange("p h s -> p (h s)")
        table_flat = TABLE[:, :, :, :].rearrange("p i q c -> p (i q c)")
        sums = [nb_flat[:, 0:NT * D], nb_flat[:, NT * D:2 * NT * D], nb_flat[:, 2 * NT * D:3 * NT * D], table_flat[:, 0:NT * D]]

        s_lx, s_lw, s_lwv, s_lwo, s_lct, s_lnb, s_lc = (sem(f"s_l{i}") for i in ("x", "w", "wv", "wo", "ct", "nb", "c"))
        s_zero, s_zt, s_zs = sem("s_zero"), sem("s_zt"), sem("s_zs")
        s_const, s_pool0, s_ge = sem("s_const"), sem("s_pool0"), sem("s_ge")
        s_st, s_mv, s_ve, s_rstd, s_xn, s_tp, s_xt = (sem(f"s_{i}") for i in ("st", "mv", "ve", "rstd", "xn", "tp", "xt"))
        s_qp, s_kp, s_vp, s_qt, s_kt, s_va = (sem(f"s_{i}") for i in ("qp", "kp", "vp", "qt", "kt", "va"))
        s_sc, s_tr, s_ex, s_pp, s_pt, s_pv = (sem(f"s_{i}") for i in ("sc", "tr", "ex", "pp", "pt", "pv"))
        s_rs, s_st1, s_ao, s_op, s_wp, s_x2 = (sem(f"s_{i}") for i in ("rs", "st1", "ao", "op", "wp", "x2"))
        s_zp, s_zs1, s_th, s_ag, s_aa, s_ap, s_yp, s_ys = (sem(f"s_{i}") for i in ("zp", "zs1", "th", "ag", "aa", "ap", "yp", "ys"))
        s_lg, s_ml, s_nm, s_el, s_re, s_pb, s_m8, s_px, s_sel, s_cum, s_cnt, s_sv, s_v8, s_eq, s_dt, s_cw = (
            sem(f"s_{i}") for i in ("lg", "ml", "nm", "el", "re", "pb", "m8", "px", "sel", "cum", "cnt", "sv", "v8", "eq", "dt", "cw"))
        s_rd = sem("s_rd")
        s_tab = [sem(f"s_tab{i}") for i in range(CHAINS)]
        s_lt, s_cn, s_ni, s_stt, s_m, s_cb, s_oh, s_iw, s_plan = (sem(f"s_{i}") for i in ("lt", "cn", "ni", "stt", "m", "cb", "oh", "iw", "plan"))
        def sems(name):
            return [sem(f"{name}{i}") for i in range(CHAINS)]

        s_ig0, s_ig, s_is = sem("s_ig0"), sem("s_ig"), sems("s_is")
        s_xr, s_w, s_add, s_et, s_ext, s_gu, s_sg, s_h, s_o, s_ob = (
            sems(f"s_{i}") for i in ("xr", "w", "add", "et", "ext", "gu", "sg", "h", "o", "ob"))
        s_fl, s_fin, s_out = sems("s_fl"), sem("s_fin"), sem("s_out")
        s_fs = sem("s_fs")

        counted = {}

        def count_for(eng, *semaphores):
            for s in semaphores:
                counted[eng, s] = eng.alloc_register(f"count_{s.name}")
                eng.reg_mov(counted[eng, s], 0)

        def wait_counted(eng, *semaphores, of=None):
            eng.wait_ge(s_lc, 64)
            for s in semaphores:
                eng.wait_ge(s, counted[eng, of or s])

        def count(eng, s, by):
            eng.reg_add(counted[eng, s], counted[eng, s], by)

        xv = x.rearrange("(n p) d -> p n d", p=P)
        block = ctx.enter_context(nc.Block())

        @block.sync
        def _(sp):
            sp.dma_start(X[:, :, :], xv).then_inc(s_lx, 16)
            sp.dma_start(C[:, :], consts).then_inc(s_lc, 16)
            sp.dma_start(TID[:, :], tok_ids).then_inc(s_lc, 16)
            sp.dma_start(BROW[:, :, :], rows.partition_broadcast(P)).then_inc(s_lc, 16)
            sp.dma_start(BQK[:, :, :], bqk).then_inc(s_lc, 16)
            sp.dma_start(WQK[:, :, :, :], wqk.rearrange("(k p) a m -> p k a m", p=P)).then_inc(s_lw, 16)
            sp.dma_start(WV[:, :, :], wv.rearrange("(k p) m -> p k m", p=P)).then_inc(s_lwv, 16)
            sp.dma_start(NB[:, :, :], neg_bias).then_inc(s_lnb, 16)
            sp.dma_start(WO[:, :, :], wo.rearrange("(k p) m -> p k m", p=P)).then_inc(s_lwo, 16)
            sp.dma_start(CT[:, :, :], ctx_t.rearrange("(k p) m -> p k m", p=P)).then_inc(s_lct, 16)
            sp.dma_start(GT[:, :, :], gate_t.rearrange("(k p) m -> p k m", p=P)).then_inc(s_lct, 16)
            sp.wait_ge(s_zero, 1)
            for i in range(CHAINS):
                sp.dma_start(table_dram[i].rearrange("(p r) c -> p (r c)", p=P), ZERO[:, 0:E * CAP * 2 // P]).then_inc(s_zt, 16)
                sp.dma_start(sums_dram[i].rearrange("(p r) d -> p (r d)", p=P), ZERO[:, 0:TOK * D // P]).then_inc(s_zs, 16)
            with sp.Fori(0, B) as b:
                sp.wait_ge(s_xn, (b * 3 + 3) * TB)
                sp.dma_start(rows_dram.rearrange("(b n p) d -> b p n d", p=P, n=TB)[bass.ds(b, 1)].rearrange("b p n d -> p (b n) d"),
                             XN[:, :, :]).then_inc(s_rd, 16)
            for i in range(CHAINS):
                sp.wait_ge(s_tab[i], 16 * NT * TOPK // CHAINS)
                sp.dma_start(TABLE[:, i, :, :], table_dram[i].rearrange("(q p s) c -> p q (s c)", p=P, s=P)).then_inc(s_lt, 16)
            sp.wait_ge(s_plan, 1)
            quads = sp.value_load(NQI[0:1, 0:1], min_val=1, max_val=MAXT // CHAINS)
            with sp.Fori(0, quads) as q:
                for i in range(CHAINS):
                    e = sp.value_load(EJ[0:1, 0, bass.ds(q * CHAINS + i, 1)], min_val=0, max_val=E - 1)
                    sp.wait_ge(s_o[i], q)
                    sp.dma_start(W13[:, i, :, :], w13_t[bass.ds(e, 1)].rearrange("e (k p) m -> p (e k) m", p=P)).then_inc(s_w[i], 16)
                    sp.dma_start(W2[:, i, :], w2_t[bass.ds(e, 1)].rearrange("e p m -> p (e m)")).then_inc(s_w[i], 16)
            for i in range(CHAINS):
                sp.wait_ge(s_add[i], quads * 16)
                sp.dma_start(sums[i].rearrange("p (n d) -> p n d", d=D), sums_dram[i].rearrange("(n p) d -> p n d", p=P)).then_inc(s_fl[i], 16)
            sp.wait_ge(s_fin, 1)
            sp.dma_start(out.rearrange("(n p) d -> p n d", p=P), X3[:, :, :]).then_inc(s_out, 16)
            sp.wait_ge(s_out, 16)

        @block.gpsimd
        def _(pool):
            count_for(pool, s_mv, s_dt, s_ig, s_add[0], *s_tab)
            pool.memset(ZERO[:, :], 0.0).then_inc(s_zero, 1)
            pool.memset(NEGH[:, :], -0.5).then_inc(s_pool0, 1)
            pool.memset(CNT[:, :], 0.0).then_inc(s_pool0, 1)
            pool.memset(VA[:, :, :, :], 1.0).then_inc(s_pool0, 1)
            pool.memset(XR[:, :, :], 0.0).then_inc(s_pool0, 1)
            pool.memset(ONES[:, :], 1.0).then_inc(s_pool0, 1)
            pool.memset(ONEF[:, :], 1.0).then_inc(s_pool0, 1)
            pool.wait_ge(s_lc, 64)
            pool.tensor_copy(TRI[:, :], C[:, C_TRI:C_TRI + P]).then_inc(s_pool0, 1)
            pool.tensor_scalar(BQN[:, :], BQK[:, 0, :], -(HD ** -0.5), None, ALU.mult).then_inc(s_pool0, 1)

            with pool.Fori(0, B) as b:
                def rstd(n):
                    count(pool, s_mv, TB)
                    wait_counted(pool, s_mv)
                    pool.tensor_scalar(VE[:, :], MV[:, :, 1], EPS, None, ALU.add).then_inc(s_ve, 1)
                    pool.wait_ge(s_ve, b * 3 + n + 1)
                    pool.tensor_tensor(RSTD[:, :], VE[:, :], NEGH[:, :], ALU.pow).then_inc(s_rstd, 1)

                rstd(0)
                for t in range(TB):
                    pool.wait_ge(s_lx, 16)
                    pool.tensor_tensor(XB[:, bass.ds(b * TB + t, 1), :].rearrange("p n d -> p (n d)"), X[:, bass.ds(b * TB + t, 1), :].rearrange("p n d -> p (n d)"),
                                       BROW[:, 1, :], ALU.add).then_inc(s_rs, 1)
                rstd(1)
                rstd(2)
                pool.wait_ge(s_zt, 16 * CHAINS)
                count(pool, s_dt, 3)
                wait_counted(pool, s_dt)
                for k in range(TOPK):
                    for t in range(TB):
                        n = k * TB + t
                        i = n % CHAINS
                        wait_counted(pool, s_tab[i])
                        pool.indirect_dma_start(out=table_dram[i], out_offset=bass.IndirectOffsetOnAxis(ap=IX[:, t, k:k + 1].bitcast(U32), axis=0),
                                                in_=DT[:, t, k, :], in_offset=None).then_inc(s_tab[i], 16)
                        count(pool, s_tab[i], 16)

            pool.wait_ge(s_plan, 1)
            quads = pool.value_load(NQI[0:1, 0:1], min_val=1, max_val=MAXT // CHAINS)
            pool.wait_ge(s_rd, 16 * B)
            pool.wait_ge(s_zs, 16 * CHAINS)

            def gather(i):
                pool.indirect_dma_start(out=XR[:, i, :], out_offset=None, in_=rows_dram,
                                        in_offset=bass.IndirectOffsetOnAxis(ap=IG[:, i:i + 1].bitcast(U32), axis=0),
                                        bounds_check=TOK - 1, oob_is_err=False).then_inc(s_xr[i], 16)

            pool.wait_ge(s_ig0, 1)
            for i in range(CHAINS):
                gather(i)
            with pool.Fori(0, quads) as q:
                count(pool, s_ig, 1)
                for i in range(CHAINS):
                    wait_counted(pool, s_ig, s_et[i], of=s_ig)
                    gather(i)
                    wait_counted(pool, s_ob[i], s_is[i], of=s_ig)
                    wait_counted(pool, s_add[i], of=s_add[0])
                    pool.indirect_dma_start(out=sums_dram[i], out_offset=bass.IndirectOffsetOnAxis(ap=IS[:, i:i + 1].bitcast(U32), axis=0),
                                            in_=OB[:, i, :], in_offset=None, bounds_check=TOK - 1, oob_is_err=False,
                                            compute_op=ALU.add).then_inc(s_add[i], 16)
                count(pool, s_add[0], 16)
            for i in range(CHAINS):
                pool.wait_ge(s_xr[i], quads * 16 + 16)

        @block.scalar
        def _(act):
            act.wait_ge(s_pool0, 8)
            with act.Fori(0, B) as b:
                def rows_t(n, dst):
                    act.wait_ge(s_tp, b * 4 + n + 1)
                    act.activation(dst[:, :, :], ps[:, 7, :].rearrange("p (k s) -> p k s", k=KD), ACT.Copy).then_inc(s_xt, 1)

                rows_t(0, XT)
                for g in range(NG):
                    act.wait_ge(s_qp, b * NG + g // 2 * 2 + 2)
                    act.activation(QT[:, g, :], ps[:, g // 2, (g % 2) * S:(g % 2 + 1) * S], ACT.Identity,
                                   bias=BQN[:, g:g + 1], scale=-(HD ** -0.5)).then_inc(s_qt, 1)
                for h in range(H):
                    act.wait_ge(s_tr, (b * H + h + 1) * 2)
                    if h >= 2:
                        act.wait_ge(s_pp, b * H + h - 1)
                    for n in range(2):
                        lo, hi = (0, P) if n == 0 else (P, SC)
                        act.activation(PR[:, h % 2, lo:hi], ps[:, h % 3, lo:hi], ACT.Exp, bias=MN[:, h, n:n + 1], scale=-1.0).then_inc(s_ex, 1)
                act.wait_ge(s_op, b + 1)
                act.activation(XT[:, :, :], ps[:, 7, :].rearrange("p (k s) -> p k s", k=KD), ACT.Copy).then_inc(s_xt, 1)
                rows_t(1, XT)
                for t in range(TB):
                    act.wait_ge(s_zs1, (b * EX + EX - 1) * TB + t + 1)
                    act.activation(TH[:, t, :], Z[:, t, :], ACT.Tanh, scale=0.5).then_inc(s_th, 1)
                rows_t(2, XT)
                rows_t(3, XT)
                for t in range(TB):
                    act.wait_ge(s_nm, b + 1)
                    act.activation(EL[:, t, :], ps[:, 6, t * E:(t + 1) * E], ACT.Exp, bias=NM[:, t:t + 1], accum_out=SE[:, t:t + 1]).then_inc(s_el, 1)

            act.wait_ge(s_plan, 1)
            quads = act.value_load(NQI[0:1, 0:1], min_val=1, max_val=MAXT // CHAINS)
            with act.Fori(0, quads) as q:
                for i in range(CHAINS + 1):
                    if i < CHAINS:
                        act.wait_ge(s_gu[i], q + 1)
                        act.activation(SG[:, i, :], ps[:, 2 + i % 2, 0:P], ACT.Silu).then_inc(s_sg[i], 1)
                    if i >= 1:
                        j = i - 1
                        act.wait_ge(s_o[j], q + 1)
                        act.wait_ge(s_add[j], q * 16)
                        act.activation(OB[:, j, :], ps[:, 4 + j % 2, 0:D], ACT.Copy,
                                       scale=IW[:, bass.ds(q * CHAINS + j, 1), 1]).then_inc(s_ob[j], 1)

        @block.tensor
        def _(pe):
            pe.wait_ge(s_lc, 64)

            with pe.Fori(0, B) as b:
                def turn(src):
                    for t in range(TB):
                        for k in range(KD):
                            last = pe.transpose(ps[:, 7, k * S + t * P:k * S + (t + 1) * P], src(t, k), ident)
                    return last

                def normed(n, ln):
                    pe.wait_ge(s_xn, (b * 3 + ln + 1) * TB)
                    turn(lambda t, k: XN[:, t, k * P:(k + 1) * P]).then_inc(s_tp, 1)

                pe.wait_ge(s_lg, b)
                normed(0, 0)
                pe.wait_ge(s_xt, b * 5 + 1)
                pe.wait_ge(s_lw, 16)
                pe.wait_ge(s_el, b * TB)
                for a in range(2):
                    for g in range(NG):
                        for k in range(KD):
                            last = pe.matmul(ps[:, 2 * a + g // 2, (g % 2) * S:(g % 2 + 1) * S], WQK[:, k, a, g * P:(g + 1) * P],
                                             XT[:, k, :], start=(k == 0), stop=(k == KD - 1))
                        last.then_inc(s_kp if a else s_qp, 1)
                pe.wait_ge(s_lwv, 16)
                for t in range(TB):
                    for k in range(KD):
                        last = pe.matmul(ps[:, 4, t * D:(t + 1) * D], XT[:, k, t * P:(t + 1) * P], WV[:, k, :],
                                         start=(k == 0), stop=(k == KD - 1))
                last.then_inc(s_vp, 1)
                pe.wait_ge(s_qt, (b + 1) * NG)
                pe.wait_ge(s_kt, (b + 1) * NG)
                for h in range(H + 2):
                    if h < H:
                        if h >= 3:
                            pe.wait_ge(s_ex, (b * H + h - 2) * 2)
                        g, lo = h // GH, (h % GH) * SLOT
                        q, k = QT[lo:lo + SLOT, g, :], KT[lo:lo + SLOT, g, :]
                        pe.matmul(ps[:, h % 3, 0:P], q[:, 0:P], k[:, 0:P], start=True, stop=True, tile_position=(lo, 0))
                        pe.matmul(ps[:, h % 3, P:SC], q[:, P:S], k[:, 0:S], start=True, stop=True, tile_position=(lo, 0)).then_inc(s_sc, 1)
                    if 1 <= h <= H:
                        j = h - 1
                        pe.wait_ge(s_ex, (b * H + j + 1) * 2)
                        if j >= 2:
                            pe.wait_ge(s_pt, b * H + j - 1)
                        else:
                            pe.wait_ge(s_va, b + 1)
                        for c in range(3):
                            last = pe.transpose(ps[:, 3 + j % 2, c * P:(c + 1) * P], PR[:, j % 2, c * P:(c + 1) * P], ident)
                        last.then_inc(s_pp, 1)
                    if h >= 2:
                        j = h - 2
                        pe.wait_ge(s_pt, b * H + j + 1)
                        pe.matmul(ps[:, 5, j * HV:(j + 1) * HV], PT[:, j % 2, 0:P], VA[:, 0, j, :], start=True, stop=True)
                        pe.matmul(ps[:, 6, j * HV:(j + 1) * HV], PT[:, j % 2, P:2 * P], VA[:, 0, j, :], start=True, stop=False)
                        pe.matmul(ps[:, 6, j * HV:(j + 1) * HV], PT[:, j % 2, 2 * P:3 * P], VA[:, 1, j, :], start=False, stop=True).then_inc(s_pv, 1)
                pe.wait_ge(s_ao, (b + 1) * TB)
                turn(lambda t, k: AO[:, t, k * 8:(k + 1) * 8, :].rearrange("p h d -> p (h d)")).then_inc(s_op, 1)
                pe.wait_ge(s_xt, b * 5 + 2)
                pe.wait_ge(s_lwo, 16)
                for t in range(TB):
                    for k in range(KD):
                        last = pe.matmul(ps[:, 4, t * D:(t + 1) * D], XT[:, k, t * P:(t + 1) * P], WO[:, k, :],
                                         start=(k == 0), stop=(k == KD - 1))
                last.then_inc(s_wp, 1)
                normed(1, 1)
                pe.wait_ge(s_xt, b * 5 + 3)
                pe.wait_ge(s_lct, 32)

                def all_experts(done):
                    for t in range(TB):
                        for n in range(2):
                            for k in range(KD):
                                last = pe.matmul(ps[:, 2 * t + n, :], XT[:, k, t * P:(t + 1) * P], CT[:, k, n * 512:(n + 1) * 512],
                                                 start=(k == 0), stop=(k == KD - 1))
                        last.then_inc(done, 1)

                all_experts(s_zp)
                pe.wait_ge(s_aa, (b + 1) * TB)
                turn(lambda t, k: AA[:, t, k * P:(k + 1) * P]).then_inc(s_tp, 1)
                pe.wait_ge(s_xt, b * 5 + 4)
                all_experts(s_yp)
                normed(3, 2)
                pe.wait_ge(s_xt, b * 5 + 5)
                for t in range(TB):
                    for k in range(KD):
                        last = pe.matmul(ps[:, 6, t * E:(t + 1) * E], XT[:, k, t * P:(t + 1) * P], GT[:, k, :],
                                         start=(k == 0), stop=(k == KD - 1))
                last.then_inc(s_lg, 1)
                pe.wait_ge(s_sel, (b + 1) * TB)
                for t in range(TB):
                    o = ps[:, 5, t * E:(t + 1) * E]
                    pe.matmul(o, TRI[:, :], SELB[:, t, :], start=True, stop=False)
                    if t == 1:
                        pe.matmul(o, ONES[:, :], SELB[:, 0, :], start=False, stop=False)
                    pe.wait_ge(s_cnt, b * TB)
                    pe.matmul(o, ONES[:, :], CNT[:, :], start=False, stop=True).then_inc(s_cum, 1)

            pe.wait_ge(s_cnt, B * TB)
            pe.matmul(ps[0:E, 0, 0:1], CNT[:, :], ONES[:, 0:1], start=True, stop=True).then_inc(s_cn, 1)
            pe.wait_ge(s_ni, 3)
            pe.matmul(ps[0:E, 0, 1:2], TRI[0:E, 0:E], NBF[:, :], start=True, stop=True)
            pe.matmul(ps[:, 0, 2:3], ONES[0:E, :], NBF[:, :], start=True, stop=True).then_inc(s_cn, 1)
            pe.wait_ge(s_m, 3)
            pe.matmul(ps[:, 1, 0:P], ONEF[0:E, :], M1[:, :], start=True, stop=True).then_inc(s_cn, 1)
            pe.wait_ge(s_oh, NQ)
            pe.wait_ge(s_lt, 16 * CHAINS)
            for c in range(2):
                for i in range(CHAINS):
                    for n in range(NQ):
                        last = pe.matmul(ps[:, 2, c * P:(c + 1) * P], TABLE[:, i, n, :].rearrange("p (s c) -> p s c", c=2)[:, :, c],
                                         OH[:, n, :], start=(i == 0 and n == 0), stop=(i == CHAINS - 1 and n == NQ - 1))
            last.then_inc(s_cn, 1)

            pe.wait_ge(s_plan, 1)
            quads = pe.value_load(NQI[0:1, 0:1], min_val=1, max_val=MAXT // CHAINS)
            with pe.Fori(0, quads) as q:
                def before(i):
                    return (i - 2) % CHAINS, q + (1 if i >= 2 else 0)

                def rows_turned(i):
                    pe.wait_ge(s_xr[i], q * 16 + 16)
                    j, n = before(i)
                    pe.wait_ge(s_ext[j], n)
                    for k in range(KD):
                        last = pe.transpose(ps[:, i % 2, k * P:(k + 1) * P], XR[:, i, k * P:(k + 1) * P], ident)
                    last.then_inc(s_et[i], 1)

                def up(i):
                    pe.wait_ge(s_w[i], q * 32 + 32)
                    pe.wait_ge(s_ext[i], q + 1)
                    j, n = before(i)
                    pe.wait_ge(s_h[j], n)
                    for c in range(2):
                        for k in range(KD):
                            last = pe.matmul(ps[:, 2 + i % 2, c * P:(c + 1) * P], W13[:, i, k, c * F:(c + 1) * F], XRT[:, i, k, :],
                                             start=(k == 0), stop=(k == KD - 1))
                    last.then_inc(s_gu[i], 1)

                def down(i):
                    pe.wait_ge(s_h[i], q + 1)
                    j, n = before(i)
                    pe.wait_ge(s_ob[j], n)
                    pe.matmul(ps[:, 4 + i % 2, 0:D], HT[:, i, :], W2[:, i, :], start=True, stop=True).then_inc(s_o[i], 1)

                for i in range(CHAINS + 2):
                    if i < CHAINS:
                        rows_turned(i)
                    if 1 <= i <= CHAINS:
                        up(i - 1)
                    if i >= 2:
                        down(i - 2)

        @block.vector
        def _(dve):
            count_for(dve, s_st, s_sc, s_ys, s_lg, s_pb, s_m8, s_sv)
            dve.wait_ge(s_lc, 64)
            for n in range(3):
                dve.tensor_scalar(GE[:, n, :], TID[:, :], float(THIRD * (n + 1)), None, ALU.is_ge).then_inc(s_ge, 1)
            dve.wait_ge(s_ge, 3)
            dve.tensor_scalar(MSK[:, :, 0], GE[:, 0, :], -1.0, 1.0, ALU.mult, ALU.add).then_inc(s_ge, 1)
            dve.tensor_tensor(MSK[:, :, 1], GE[:, 0, :], GE[:, 1, :], ALU.subtract).then_inc(s_ge, 1)
            dve.tensor_tensor(MSK[:, :, 2], GE[:, 1, :], GE[:, 2, :], ALU.subtract).then_inc(s_ge, 1)
            dve.tensor_copy(MSK[:, :, 3], GE[:, 2, :]).then_inc(s_ge, 1)
            dve.wait_ge(s_ge, 7)
            dve.wait_ge(s_pool0, 8)
            dve.wait_ge(s_lx, 16)

            with dve.Fori(0, B) as b:
                def tile(buf, t, *rest):
                    return buf[:, bass.ds(b * TB + t, 1), :].rearrange("p n d -> p (n d)")

                def norm(n, src, free, made=lambda: None):
                    made()
                    for t in range(TB):
                        dve.bn_stats(ST[:, t, :], src(t)).then_inc(s_st, 1)
                    for t in range(TB):
                        count(dve, s_st, 1)
                        wait_counted(dve, s_st)
                        dve.bn_aggr(MV[:, t, :], ST[:, t, :]).then_inc(s_mv, 1)
                    dve.wait_ge(s_rstd, b * 3 + n + 1)
                    free()
                    for t in range(TB):
                        dve.tensor_scalar(XN[:, t, :], src(t), MV[:, t, 0:1], RSTD[:, t:t + 1], ALU.subtract, ALU.mult).then_inc(s_xn, 1)

                norm(0, lambda t: tile(X, t), lambda: dve.wait_ge(s_rd, b * 16))
                for g in range(NG):
                    dve.wait_ge(s_kp, b * NG + g // 2 * 2 + 2)
                    dve.tensor_scalar(KT[:, g, :], ps[:, 2 + g // 2, (g % 2) * S:(g % 2 + 1) * S], BQK[:, 1, g:g + 1], None,
                                      ALU.add).then_inc(s_kt, 1)
                dve.wait_ge(s_vp, b + 1)
                for t in range(TB):
                    last = dve.tensor_tensor(VA[:, t, :, 0:HD], ps[:, 4, t * D:(t + 1) * D].rearrange("p (h d) -> p h d", h=H),
                                             BROW[:, 0, :].rearrange("p (h d) -> p h d", h=H), ALU.add)
                last.then_inc(s_va, 1)
                dve.wait_ge(s_lnb, 16)
                for h in range(H + 1):
                    if h < H:
                        count(dve, s_sc, 1)
                        wait_counted(dve, s_sc)
                        for n in range(2):
                            lo, hi = (0, P) if n == 0 else (P, SC)
                            dve.tensor_tensor_reduce(ps[:, h % 3, lo:hi], ps[:, h % 3, lo:hi], NB[:, h, lo:hi], 1.0, 3e38, ALU.add, ALU.min,
                                                     MN[:, h, n:n + 1]).then_inc(s_tr, 1)
                    if h >= 1:
                        j = h - 1
                        dve.wait_ge(s_pp, b * H + j + 1)
                        if j >= 2:
                            dve.wait_ge(s_pv, b * H + j - 1)
                        dve.tensor_copy(PT[:, j % 2, :], ps[:, 3 + j % 2, 0:SC]).then_inc(s_pt, 1)
                dve.wait_ge(s_pv, (b + 1) * H)
                for t in range(TB):
                    o = ps[:, 5 + t, 0:H * HV].rearrange("p (h d) -> p h d", h=H)
                    dve.reciprocal(RS[:, t, :], o[:, :, HD]).then_inc(s_st1, 1)
                for t in range(TB):
                    o = ps[:, 5 + t, 0:H * HV].rearrange("p (h d) -> p h d", h=H)
                    dve.wait_ge(s_st1, b * TB + t + 1)
                    dve.tensor_tensor(AO[:, t, :, :], o[:, :, 0:HD], RS[:, t, :].unsqueeze(2).to_broadcast([P, H, HD]), ALU.mult).then_inc(s_ao, 1)
                dve.wait_ge(s_wp, b + 1)
                dve.wait_ge(s_rs, (b + 1) * TB)
                for t in range(TB):
                    dve.tensor_tensor(X2[:, t, :], ps[:, 4, t * D:(t + 1) * D], tile(XB, t), ALU.add).then_inc(s_x2, 1)
                norm(1, lambda t: X2[:, t, :], lambda: None, lambda: dve.wait_ge(s_x2, (b + 1) * TB))

                def mask(t, e):
                    return MSK[:, bass.ds(b * TB + t, 1), e]

                for e in range(EX):
                    for t in range(TB):
                        if e == 0:
                            dve.wait_ge(s_zp, b * TB + t + 1)
                            dve.tensor_scalar(Z[:, t, :], ps[:, 2 * t, 0:D], mask(t, e), None, ALU.mult).then_inc(s_zs1, 1)
                        else:
                            dve.wait_ge(s_zs1, b * TB * EX + e * TB + t - 1)
                            dve.scalar_tensor_tensor(Z[:, t, :], ps[:, 2 * t + e // 2, (e % 2) * D:(e % 2 + 1) * D], mask(t, e), Z[:, t, :],
                                                     ALU.mult, ALU.add).then_inc(s_zs1, 1)
                for t in range(TB):
                    dve.wait_ge(s_th, b * TB + t + 1)
                    dve.scalar_tensor_tensor(AA[:, t, :], TH[:, t, :], 1.0, Z[:, t, :], ALU.add, ALU.mult).then_inc(s_ag, 1)
                for t in range(TB):
                    dve.wait_ge(s_ag, b * TB + t + 1)
                    dve.scalar_tensor_tensor(AA[:, t, :], AA[:, t, :], 0.5, Z[:, t, :], ALU.mult, ALU.mult).then_inc(s_aa, 1)
                for e in range(EX):
                    for t in range(TB):
                        if e == 0:
                            dve.wait_ge(s_yp, b * TB + t + 1)
                        else:
                            dve.wait_ge(s_ys, b * TB * EX + e * TB + t - 1)
                        dve.scalar_tensor_tensor(tile(X3, t), ps[:, 2 * t + e // 2, (e % 2) * D:(e % 2 + 1) * D], mask(t, e),
                                                 X2[:, t, :] if e == 0 else tile(X3, t), ALU.mult, ALU.add).then_inc(s_ys, 1)
                count(dve, s_ys, TB * EX)
                norm(2, lambda t: tile(X3, t), lambda: None, lambda: wait_counted(dve, s_ys))

                count(dve, s_lg, 1)
                wait_counted(dve, s_lg)
                for t in range(TB):
                    dve.max(ML[:, t, :], ps[:, 6, t * E:(t + 1) * E]).then_inc(s_ml, 1)
                dve.wait_ge(s_ml, (b + 1) * TB)
                dve.tensor_scalar(NM[:, :], ML[:, :, 0], -1.0, None, ALU.mult).then_inc(s_nm, 1)
                dve.wait_ge(s_el, (b + 1) * TB)
                dve.reciprocal(RE[:, :], SE[:, :]).then_inc(s_re, 1)
                dve.wait_ge(s_re, b + 1)
                for t in range(TB):
                    dve.tensor_scalar(PB[:, t, :], EL[:, t, :], RE[:, t:t + 1], None, ALU.mult).then_inc(s_pb, 1)
                for t in range(TB):
                    count(dve, s_pb, 1)
                    wait_counted(dve, s_pb)
                    dve.max(M8[:, t, :], PB[:, t, :]).then_inc(s_m8, 1)
                for t in range(TB):
                    count(dve, s_m8, 1)
                    wait_counted(dve, s_m8)
                    dve.match_replace(PX[:, t, :], M8[:, t, :], PB[:, t, :], -1.0).then_inc(s_px, 1)
                for t in range(TB):
                    dve.wait_ge(s_px, b * TB + t + 1)
                    dve.tensor_scalar(SELB[:, t, :], PX[:, t, :], 0.0, None, ALU.is_lt).then_inc(s_sel, 1)
                for t in range(TB):
                    dve.tensor_scalar(SEL[:, t, :], PX[:, t, :], 0.0, None, ALU.is_lt).then_inc(s_eq, 1)
                dve.wait_ge(s_eq, b * 4 + 2)
                dve.tensor_tensor(CW[:, :, :], PB[:, :, :], SEL[:, :, :], ALU.mult).then_inc(s_cw, 1)
                dve.wait_ge(s_cum, (b + 1) * TB)
                for t in range(TB):
                    dve.wait_ge(s_cnt, b * TB + t)
                    dve.tensor_tensor(CNT[:, :], CNT[:, :], SELB[:, t, :], ALU.add).then_inc(s_cnt, 1)
                for t in range(TB):
                    dve.tensor_tensor(SV[:, t, :], ps[:, 5, t * E:(t + 1) * E], C[:, C_SLOT:C_SLOT + E], ALU.add).then_inc(s_sv, 1)
                dve.wait_ge(s_sv, b * 3 + 2)
                dve.tensor_tensor(SV[:, :, :], SV[:, :, :], SEL[:, :, :], ALU.mult).then_inc(s_sv, 1)
                count(dve, s_sv, 3)
                wait_counted(dve, s_sv)
                for t in range(TB):
                    dve.max(V8[:, t, :], SV[:, t, :]).then_inc(s_v8, 1)
                dve.wait_ge(s_v8, (b + 1) * TB)
                for i in range(CHAINS):
                    dve.wait_ge(s_tab[i], b * 16 * (TB * TOPK // CHAINS))
                dve.tensor_scalar(IX[:, :, :], V8[:, :, :], -1.0, None, ALU.add).then_inc(s_dt, 1)
                dve.tensor_tensor(EQ[:, :, :, :], V8[:, :, :].unsqueeze(3).to_broadcast([P, TB, TOPK, E]),
                                  SV[:, :, :].unsqueeze(2).to_broadcast([P, TB, TOPK, E]), ALU.is_equal).then_inc(s_eq, 1)
                dve.wait_ge(s_eq, b * 4 + 3)
                dve.wait_ge(s_cw, b + 1)
                dve.tensor_tensor(EQ[:, :, :, :], EQ[:, :, :, :], CW[:, :, :].unsqueeze(2).to_broadcast([P, TB, TOPK, E]), ALU.mult).then_inc(s_eq, 1)
                dve.tensor_copy(DT[:, :, :, 0], C[:, bass.ds(b * TB + C_TOK, TB)].unsqueeze(2).to_broadcast([P, TB, TOPK])).then_inc(s_dt, 1)
                dve.wait_ge(s_eq, b * 4 + 4)
                dve.tensor_reduce(DT[:, :, :, 1], EQ[:, :, :, :], AX_X, ALU.add).then_inc(s_dt, 1)

            dve.wait_ge(s_cn, 1)
            dve.tensor_scalar(NI[:, 0:1], ps[0:E, 0, 0:1], float(P - 1), None, ALU.add).then_inc(s_ni, 1)
            dve.wait_ge(s_ni, 1)
            dve.tensor_scalar(NI[:, 1:2], NI[:, 0:1], 7, None, ALU.logical_shift_right).then_inc(s_ni, 1)
            dve.wait_ge(s_ni, 2)
            dve.tensor_copy(NBF[:, :], NI[:, 1:2]).then_inc(s_ni, 1)
            dve.wait_ge(s_cn, 2)
            dve.tensor_copy(SN[:, 0:1], ps[0:E, 0, 1:2]).then_inc(s_stt, 1)
            dve.tensor_copy(NTF[:, :], ps[:, 0, 2:3]).then_inc(s_stt, 1)
            dve.wait_ge(s_ni, 3)
            dve.tensor_tensor(SN[:, 1:2], ps[0:E, 0, 1:2], NBF[:, :], ALU.add).then_inc(s_stt, 1)
            dve.tensor_tensor(SN[:, 2:3], C[0:E, C_E8:C_E8 + 1], ps[0:E, 0, 1:2], ALU.subtract).then_inc(s_stt, 1)
            dve.wait_ge(s_stt, 4)
            dve.tensor_scalar(M1[:, :], C[0:E, C_IOTA:C_IOTA + P], SN[:, 2:3], None, ALU.add).then_inc(s_m, 1)
            dve.wait_ge(s_m, 1)
            dve.scalar_tensor_tensor(M2[:, :], C[0:E, C_IOTA:C_IOTA + P], SN[:, 0:1], M1[:, :], ALU.is_ge, ALU.mult).then_inc(s_m, 1)
            dve.wait_ge(s_m, 2)
            dve.scalar_tensor_tensor(M1[:, :], C[0:E, C_IOTA:C_IOTA + P], SN[:, 1:2], M2[:, :], ALU.is_lt, ALU.mult).then_inc(s_m, 1)
            dve.tensor_scalar(LATE[:, :], iota, NTF[:, 0:1], 8.0 * TOK, ALU.is_ge, ALU.mult).then_inc(s_cb, 1)
            dve.tensor_scalar(NQI[0:1, 1:2], NTF[0:1, :], float(CHAINS - 1), None, ALU.add).then_inc(s_cb, 1)
            dve.wait_ge(s_cn, 3)
            dve.wait_ge(s_cb, 2)
            dve.tensor_tensor(CB[:, :], LATE[:, :], ps[:, 1, 0:P], ALU.add).then_inc(s_cb, 1)
            dve.tensor_scalar(NQI[0:1, 0:1], NQI[0:1, 1:2], 2, None, ALU.logical_shift_right).then_inc(s_cb, 1)
            dve.wait_ge(s_cb, 4)
            for n in range(NQ):
                dve.tensor_scalar(OH[:, n, :], CB[:, :], C[:, C_PQ + n:C_PQ + n + 1], None, ALU.is_equal).then_inc(s_oh, 1)
            dve.tensor_scalar(EJ[:, 1, :], CB[0:1, :], 8.0 * E - 1, None, ALU.min).then_inc(s_cb, 1)
            dve.wait_ge(s_cb, 5)
            dve.tensor_scalar(EJ[:, 0, :], EJ[:, 1, :], 3, None, ALU.logical_shift_right).then_inc(s_cb, 1)
            dve.wait_ge(s_cb, 6)
            dve.memset(IW[:, MAXT:MAXT + CHAINS, :], float(EMPTY)).then_inc(s_iw, 1)
            dve.wait_ge(s_cn, 4)
            dve.tensor_scalar(IW[:, 0:MAXT, 0], ps[:, 2, 0:P], float(EMPTY), None, ALU.add).then_inc(s_iw, 1)
            dve.tensor_copy(IW[:, 0:MAXT, 1], ps[:, 2, P:2 * P]).then_inc(s_iw, 1)
            dve.wait_ge(s_iw, 3)
            dve.tensor_copy(IG[:, :], IW[:, 0:CHAINS, 0]).then_inc(s_ig0, 1)
            dve.engine_nop().then_inc(s_plan, 1)

            quads = dve.value_load(NQI[0:1, 0:1], min_val=1, max_val=MAXT // CHAINS)
            with dve.Fori(0, quads) as q:
                def rows_out(i):
                    dve.wait_ge(s_et[i], q + 1)
                    dve.tensor_copy(XRT[:, i, :, :], ps[:, i % 2, 0:KD * P].rearrange("p (k s) -> p k s", k=KD)).then_inc(s_ext[i], 1)
                    dve.wait_ge(s_add[i], q * 16)
                    dve.tensor_copy(IS[:, i:i + 1], IW[:, bass.ds(q * CHAINS + i, 1), 0]).then_inc(s_is[i], 1)

                for i in range(CHAINS + 1):
                    if i < CHAINS:
                        rows_out(i)
                    if i == 0:
                        for n in range(CHAINS):
                            dve.wait_ge(s_xr[n], q * 16 + 16)
                        dve.tensor_copy(IG[:, :], IW[:, bass.ds(q * CHAINS + CHAINS, CHAINS), 0]).then_inc(s_ig, 1)
                    if i >= 1:
                        j = i - 1
                        dve.wait_ge(s_sg[j], q + 1)
                        dve.tensor_tensor(HT[:, j, :], ps[:, 2 + j % 2, P:2 * P], SG[:, j, :], ALU.mult).then_inc(s_h[j], 1)

            x3 = X3[:, :, :].rearrange("p n d -> p (n d)")
            for i in range(CHAINS):
                dve.wait_ge(s_fl[i], 16)
                if i:
                    dve.wait_ge(s_fs, i)
                dve.tensor_tensor(x3, x3, sums[i], ALU.add).then_inc(s_fin if i == CHAINS - 1 else s_fs, 1)


def _consts():
    import numpy as np

    c = np.zeros((P, C_W), np.float32)
    p, j = np.arange(P)[:, None], np.arange(P)[None, :]
    c[:, C_ID:C_ID + P] = p == j
    c[:, C_TRI:C_TRI + P] = p < j
    c[:, C_IOTA:C_IOTA + P] = j
    c[:, C_PQ:C_PQ + NQ] = p + P * np.arange(NQ)
    c[:, C_SLOT:C_SLOT + E] = CAP * np.arange(E) + 1
    c[:, C_TOK:C_TOK + NT] = p + P * np.arange(NT) - EMPTY
    c[:, C_E8] = CAP // P * np.arange(P)
    start = 2 ** (-2 ** (-(np.log2(H) - 3)))
    slopes = np.array([start * start ** i for i in range(H)], np.float32)
    key = np.concatenate([np.arange(P), np.arange(S)])
    query = np.arange(P)[:, None] + np.where(np.arange(SC) < P, 0, P)
    nb = slopes[None, :, None] * (S - 1 - key).astype(np.float32)[None, None, :]
    nb = np.where((key[None, :] > query)[:, None, :], np.float32(1e37), nb).astype(np.float32)
    return c, nb


def kernel(x, itok_BxS_13_99985, ctx_2048, L0_attn_Wq, L0_attn_bq, L0_attn_Wk, L0_attn_bk, L0_attn_Wv, L0_attn_bv,
           L0_attn_Wo, L0_attn_bo, L0_ffn_gate_w, L0_ffn_w13, L0_ffn_w2):
    import numpy as np
    import concourse.bacc as bacc
    from concourse.bass_utils import run_bass_kernel_spmd

    def slots(w, bias=False):
        w = np.asarray(w).reshape(-1, H, HD)
        out = np.zeros((w.shape[0], H, SLOT), np.float32)
        out[:, :, :HD] = w
        return out.reshape(-1, H * SLOT)

    def slot_rows(v):
        return slots(v).reshape(NG, P).T

    consts, neg_bias = _consts()
    arrays = {
        "x": np.asarray(x).reshape(TOK, D),
        "tok_ids": np.asarray(itok_BxS_13_99985).reshape(NT, P).T,
        "ctx_t": np.asarray(ctx_2048).transpose(2, 0, 1).reshape(D, EX * CTX),
        "wqk": np.stack([slots(L0_attn_Wq), slots(L0_attn_Wk)], axis=1),
        "wv": np.asarray(L0_attn_Wv),
        "wo": np.asarray(L0_attn_Wo),
        "bqk": np.stack([slot_rows(L0_attn_bq), slot_rows(L0_attn_bk)], axis=1),
        "rows": np.stack([np.asarray(L0_attn_bv), np.asarray(L0_attn_bo)]),
        "gate_t": np.asarray(L0_ffn_gate_w).T,
        "w13_t": np.asarray(L0_ffn_w13).transpose(0, 2, 1),
        "w2_t": np.asarray(L0_ffn_w2).transpose(0, 2, 1),
        "consts": consts,
        "neg_bias": neg_bias,
    }
    arrays = {k: np.ascontiguousarray(v) for k, v in arrays.items()}
    nc = bacc.Bacc("TRN2", target_bir_lowering=False, num_devices=1)
    args = [nc.dram_tensor(f"in_{k}", v.shape, mybir.dt.from_np(v.dtype), kind="ExternalInput").ap() for k, v in arrays.items()]
    out = nc.dram_tensor("out", (TOK, D), F32, kind="ExternalOutput").ap()
    decoder_kernel(nc, *args, out)
    r = run_bass_kernel_spmd(nc, [{f"in_{k}": v for k, v in arrays.items()}], core_ids=[0])
    return r.results[0]["out"].reshape(B, S, D)
```

```python
from contextlib import ExitStack

import concourse.bass as bass
from concourse import mybir

ALU = mybir.AluOpType
ACT = mybir.ActivationFunctionType
F32 = mybir.dt.float32
BF16 = mybir.dt.bfloat16
I32 = mybir.dt.int32
U32 = mybir.dt.uint32
AX_X = mybir.AxisListType.X

P = 128
B, S, D = 4, 256, 256
TOK = B * S
NT = TOK // P
TB = S // P
KD = D // P
H, HD = 16, 16
SLOT = 32
GH = P // SLOT
NG = H // GH
HV = HD + 1
SC = P + S
EX, CTX = 4, 256
THIRD = 12500 // EX
E, TOPK, F = 64, 8, 128
CAP = TOK
COLS = E * CAP // P
NQ = COLS // P
CHAINS = 4
LEAST = TOK * TOPK // P // CHAINS
MAXT = 128
EMPTY = 4096
EPS = 1e-5

PRE = {"ln1": -17, "n1": -16, "t_x": -16, "q0": -15, "q1": -14, "k0": -11, "k1": -5, "v": -4}
POST = {"t_ao": 19, "wo": 20, "ln2": 20, "n2": 21, "t_x2": 21, "z00": 22, "z01": 23, "z10": 24, "z11": 25, "a0": 25, "a1": 27, "t_a": 27,
        "y00": 28, "y01": 29, "y10": 30, "y11": 31, "ln3": 31, "n3": 32, "t_x3": 32, "lg": 33, "top": 33, "pick": 34, "cum": 35, "slot": 36,
        "scatter": 37}
AT = PRE | POST
SLOTS = range(min(PRE.values()), (B - 1) * H + max(POST.values()) + 4)
TURNS = ("t_x", "t_ao", "t_x2", "t_a", "t_x3")
UNITS = ("q0", "q1", "k0", "k1", "v", "wo", "z00", "z01", "z10", "z11", "y00", "y01", "y10", "y11", "lg", "cum")


def steps(n):
    return [(p, name) for p in range(B) for name in AT if n - p * H == AT[name]]


def numbered(names):
    return {key: i for i, key in enumerate(key for n in SLOTS for key in steps(n) if key[1] in names)}


TURN_NO = numbered(TURNS)
UNIT_NO = numbered(UNITS)
LN_NO = numbered(("ln1", "ln2", "ln3"))
C_ID, C_TRI, C_IOTA, C_PQ, C_SLOT, C_TOK, C_E8 = 0, 128, 256, 384, 388, 452, 460
C_W = 461


def decoder_kernel(nc, x, tok_ids, ctx_t, wqk, wv, wo, bqk, rows, gate_t, w13_t, w2_t, consts, neg_bias, out):
    with ExitStack() as ctx:
        def sb(name, shape, dt=F32):
            return ctx.enter_context(nc.sbuf_tensor(name, shape, dt))

        def sem(name):
            return ctx.enter_context(nc.semaphore(name))

        rows_dram = nc.dram_tensor("rows_dram", (TOK, D), F32).ap()
        table_dram = [nc.dram_tensor(f"table_dram{i}", (E * CAP, 2), F32).ap() for i in range(CHAINS)]
        sums_dram = [nc.dram_tensor(f"sums_dram{i}", (TOK, D), F32).ap() for i in range(CHAINS)]

        X = sb("X", [P, NT, D])
        XB = sb("XB", [P, NT, D])
        TID = sb("TID", [P, NT], I32)
        CT = sb("CT", [P, KD, EX * CTX])
        WQK = sb("WQK", [P, KD, 2, NG * P])
        WV = sb("WV", [P, KD, D])
        WO = sb("WO", [P, KD, D])
        BQK = sb("BQK", [P, 2, NG])
        BQN = sb("BQN", [P, NG])
        BROW = sb("BROW", [P, 2, D])
        GT = sb("GT", [P, KD, E])
        C = sb("C", [P, C_W])
        NB = sb("NB", [P, H, SC])
        ZERO = sb("ZERO", [P, 2048])
        NEGH = sb("NEGH", [P, TB])
        TRI = sb("TRI", [P, P], BF16)
        ONES = sb("ONES", [P, P], BF16)
        ONEF = sb("ONEF", [P, P])
        GE = sb("GE", [P, 3, NT])
        MSK = sb("MSK", [P, NT, EX])

        ST = sb("ST", [P, 3, TB, 6])
        MV = sb("MV", [P, 3, TB, 2])
        VE = sb("VE", [P, 3, TB])
        RSTD = sb("RSTD", [P, 3, TB])
        XN = sb("XN", [P, 3, TB, D])
        XT = sb("XT", [P, len(TURNS), KD, S])
        QT = sb("QT", [P, 2, NG, S])
        KT = sb("KT", [P, 2, NG, S])
        VA = sb("VA", [P, 2, TB, H, HV])
        MN = sb("MN", [P, 4, 2])
        PR = sb("PR", [P, 2, SC])
        PT = sb("PT", [P, 2, SC])
        RS = sb("RS", [P, TB, H])
        AO = sb("AO", [P, TB, H, HD])
        X2 = sb("X2", [P, TB, D])
        Z = sb("Z", [P, TB, CTX])
        TH = sb("TH", [P, TB, CTX])
        AA = sb("AA", [P, TB, CTX])
        X3 = sb("X3", [P, NT, D])
        ML = sb("ML", [P, TB, 8])
        NM = sb("NM", [P, TB])
        EL = sb("EL", [P, TB, E])
        SE = sb("SE", [P, TB])
        RE = sb("RE", [P, TB])
        PB = sb("PB", [P, TB, E])
        M8 = sb("M8", [P, TB, 8])
        PX = sb("PX", [P, TB, E])
        SEL = sb("SEL", [P, TB, E])
        SELB = sb("SELB", [P, TB, E], BF16)
        CNT = sb("CNT", [P, E], BF16)
        CW = sb("CW", [P, TB, E])
        SV = sb("SV", [P, TB, E])
        V8 = sb("V8", [P, TB, 8])
        IX = sb("IX", [P, TB, 8], I32)
        EQ = sb("EQ", [P, TB, 8, E])
        DT = sb("DT", [P, TB, 8, 2])

        TABLE = sb("TABLE", [P, CHAINS, NQ, P * 2])
        NI = sb("NI", [E, 4], I32)
        NBF = sb("NBF", [E, 1], BF16)
        SN = sb("SN", [E, 4])
        M1 = sb("M1", [E, P])
        M2 = sb("M2", [E, P])
        CB = sb("CB", [P, P])
        LATE = sb("LATE", [P, P])
        NTF = sb("NTF", [P, 1])
        OH = sb("OH", [P, NQ, P])
        IW = sb("IW", [P, MAXT + CHAINS, 2])
        EJ = sb("EJ", [1, 3, MAXT], I32)
        NQI = sb("NQI", [1, 4], I32)

        XR = sb("XR", [P, CHAINS, D])
        IG = sb("IG", [P, CHAINS], I32)
        IS = sb("IS", [P, CHAINS], I32)
        XRT = sb("XRT", [P, CHAINS, KD, P])
        W13 = sb("W13", [P, CHAINS, KD, 2 * F])
        W2 = sb("W2", [P, CHAINS, D])
        SG = sb("SG", [P, CHAINS, P])
        HT = sb("HT", [P, CHAINS, P])
        OB = sb("OB", [P, CHAINS, D])

        ps = ctx.enter_context(nc.psum_tensor("ps", [P, 8, 512], F32))

        ident = C[:, C_ID:C_ID + P]
        iota = C[:, C_IOTA:C_IOTA + P]
        nb_flat = NB[:, :, :].rearrange("p h s -> p (h s)")
        table_flat = TABLE[:, :, :, :].rearrange("p i q c -> p (i q c)")
        sums = [nb_flat[:, 0:NT * D], nb_flat[:, NT * D:2 * NT * D], nb_flat[:, 2 * NT * D:3 * NT * D], table_flat[:, 0:NT * D]]

        s_lx, s_lw, s_lwv, s_lwo, s_lct, s_lnb, s_lc = (sem(f"s_l{i}") for i in ("x", "w", "wv", "wo", "ct", "nb", "c"))
        s_zero, s_zt, s_zs = sem("s_zero"), sem("s_zt"), sem("s_zs")
        s_pool0, s_ge, s_xb = sem("s_pool0"), sem("s_ge"), sem("s_xb")
        s_st, s_mv, s_ve, s_rstd, s_xn = (sem(f"s_{i}") for i in ("st", "mv", "ve", "rstd", "xn"))
        s_tp, s_xt = sem("s_tp"), sem("s_xt")
        s_unit, s_used = [sem(f"s_unit{i}") for i in range(2)], [sem(f"s_used{i}") for i in range(2)]
        s_sc, s_tr, s_ex, s_pp, s_pt, s_pv = (sem(f"s_{i}") for i in ("sc", "tr", "ex", "pp", "pt", "pv"))
        s_rs, s_ao = sem("s_rs"), sem("s_ao")
        s_z, s_th, s_ag, s_aa, s_y = (sem(f"s_{i}") for i in ("z", "th", "ag", "aa", "y"))
        s_ml, s_nm, s_re, s_pb, s_m8, s_px, s_sel, s_cnt, s_sv, s_v8, s_eq, s_dt, s_cw = (
            sem(f"s_{i}") for i in ("ml", "nm", "re", "pb", "m8", "px", "sel", "cnt", "sv", "v8", "eq", "dt", "cw"))
        s_rd = sem("s_rd")
        s_tab = [sem(f"s_tab{i}") for i in range(CHAINS)]
        s_lt, s_cn, s_ni, s_stt, s_m, s_cb, s_oh, s_iw, s_plan = (sem(f"s_{i}") for i in ("lt", "cn", "ni", "stt", "m", "cb", "oh", "iw", "plan"))

        def sems(name):
            return [sem(f"{name}{i}") for i in range(CHAINS)]

        s_ig, s_xr, s_w, s_et, s_ext, s_gu, s_sg, s_h, s_o, s_ob, s_add = (
            sems(f"s_{i}") for i in ("ig", "xr", "w", "et", "ext", "gu", "sg", "h", "o", "ob", "add"))
        s_fl, s_fs, s_fin, s_out = sems("s_fl"), sem("s_fs"), sem("s_fin"), sem("s_out")

        def produced(eng, p, name):
            n = UNIT_NO[p, name]
            eng.wait_ge(s_unit[n % 2], n // 2 + 1)
            return 6 + n % 2, s_used[n % 2]

        def consumed(eng, p, name):
            n = UNIT_NO[p, name]
            eng.wait_ge(s_used[n % 2], n // 2 + 1)

        xv = x.rearrange("(n p) d -> p n d", p=P)
        block = ctx.enter_context(nc.Block())

        @block.sync
        def _(sp):
            sp.dma_start(X[:, :, :], xv).then_inc(s_lx, 16)
            sp.dma_start(C[:, :], consts).then_inc(s_lc, 16)
            sp.dma_start(TID[:, :], tok_ids).then_inc(s_lc, 16)
            sp.dma_start(BROW[:, :, :], rows.partition_broadcast(P)).then_inc(s_lc, 16)
            sp.dma_start(BQK[:, :, :], bqk).then_inc(s_lc, 16)
            sp.dma_start(WQK[:, :, :, :], wqk.rearrange("(k p) a m -> p k a m", p=P)).then_inc(s_lw, 16)
            sp.dma_start(WV[:, :, :], wv.rearrange("(k p) m -> p k m", p=P)).then_inc(s_lwv, 16)
            sp.dma_start(NB[:, :, :], neg_bias).then_inc(s_lnb, 16)
            sp.dma_start(WO[:, :, :], wo.rearrange("(k p) m -> p k m", p=P)).then_inc(s_lwo, 16)
            sp.dma_start(CT[:, :, :], ctx_t.rearrange("(k p) m -> p k m", p=P)).then_inc(s_lct, 16)
            sp.dma_start(GT[:, :, :], gate_t.rearrange("(k p) m -> p k m", p=P)).then_inc(s_lct, 16)
            sp.wait_ge(s_zero, 1)
            for i in range(CHAINS):
                sp.dma_start(table_dram[i].rearrange("(p r) c -> p (r c)", p=P), ZERO[:, 0:E * CAP * 2 // P]).then_inc(s_zt, 16)
                sp.dma_start(sums_dram[i].rearrange("(p r) d -> p (r d)", p=P), ZERO[:, 0:TOK * D // P]).then_inc(s_zs, 16)
            for b in range(B):
                sp.wait_ge(s_xn, LN_NO[b, "ln3"] * TB + TB)
                sp.dma_start(rows_dram[b * S:(b + 1) * S, :].rearrange("(n p) d -> p n d", p=P), XN[:, 2, :, :]).then_inc(s_rd, 16)
            for i in range(CHAINS):
                sp.wait_ge(s_tab[i], 16 * NT * TOPK // CHAINS)
                sp.dma_start(TABLE[:, i, :, :], table_dram[i].rearrange("(q p s) c -> p q (s c)", p=P, s=P)).then_inc(s_lt, 16)
            sp.wait_ge(s_plan, 1)
            quads = sp.value_load(NQI[0:1, 0:1], min_val=LEAST, max_val=MAXT // CHAINS)

            def load(q, i):
                e = sp.value_load(EJ[0:1, 0, bass.ds(q * CHAINS + i, 1)], min_val=0, max_val=E - 1)
                sp.dma_start(W13[:, i, :, :], w13_t[bass.ds(e, 1)].rearrange("e (k p) m -> p (e k) m", p=P)).then_inc(s_w[i], 16)
                sp.dma_start(W2[:, i, :], w2_t[bass.ds(e, 1)].rearrange("e p m -> p (e m)")).then_inc(s_w[i], 16)

            for i in range(CHAINS):
                load(0, i)
            with sp.Fori(1, quads) as q:
                for i in range(CHAINS):
                    sp.wait_ge(s_o[i], q)
                    load(q, i)
            for i in range(CHAINS):
                sp.wait_ge(s_add[i], quads * 16)
                sp.dma_start(sums[i].rearrange("p (n d) -> p n d", d=D), sums_dram[i].rearrange("(n p) d -> p n d", p=P)).then_inc(s_fl[i], 16)
            sp.wait_ge(s_fin, 1)
            sp.dma_start(out.rearrange("(n p) d -> p n d", p=P), X3[:, :, :]).then_inc(s_out, 16)
            sp.wait_ge(s_out, 16)

        @block.gpsimd
        def _(pool):
            pool.memset(ZERO[:, :], 0.0).then_inc(s_zero, 1)
            pool.memset(NEGH[:, :], -0.5).then_inc(s_pool0, 1)
            pool.memset(CNT[:, :], 0.0).then_inc(s_pool0, 1)
            pool.memset(VA[:, :, :, :, :], 1.0).then_inc(s_pool0, 1)
            pool.memset(XR[:, :, :], 0.0).then_inc(s_pool0, 1)
            pool.memset(ONES[:, :], 1.0).then_inc(s_pool0, 1)
            pool.memset(ONEF[:, :], 1.0).then_inc(s_pool0, 1)
            pool.wait_ge(s_lc, 64)
            pool.tensor_copy(TRI[:, :], C[:, C_TRI:C_TRI + P]).then_inc(s_pool0, 1)
            pool.tensor_scalar(BQN[:, :], BQK[:, 0, :], -(HD ** -0.5), None, ALU.mult).then_inc(s_pool0, 1)

            pool.wait_ge(s_lx, 16)
            for t in range(NT):
                pool.tensor_tensor(XB[:, t, :], X[:, t, :], BROW[:, 1, :], ALU.add).then_inc(s_xb, 1)

            for n in SLOTS:
                for p, name in steps(n):
                    if name in ("ln1", "ln2", "ln3"):
                        k = LN_NO[p, name]
                        pool.wait_ge(s_mv, (k + 1) * TB)
                        n3 = int(name[2]) - 1
                        pool.tensor_scalar(VE[:, n3, :], MV[:, n3, :, 1], EPS, None, ALU.add).then_inc(s_ve, 1)
                        pool.wait_ge(s_ve, k + 1)
                        pool.tensor_tensor(RSTD[:, n3, :], VE[:, n3, :], NEGH[:, :], ALU.pow).then_inc(s_rstd, 1)
                p, part = divmod(n - AT["scatter"], H)
                if 0 <= p < B and part < 4:
                    if part == 0:
                        pool.wait_ge(s_dt, (p + 1) * 3)
                        pool.wait_ge(s_zt, 16 * CHAINS)
                    for k in range(2 * part, 2 * part + 2):
                        for t in range(TB):
                            i = (k * TB + t) % CHAINS
                            m = p * (TB * TOPK // CHAINS) + (k * TB + t) // CHAINS
                            if m:
                                pool.wait_ge(s_tab[i], m * 16)
                            pool.indirect_dma_start(out=table_dram[i], out_offset=bass.IndirectOffsetOnAxis(ap=IX[:, t, k:k + 1].bitcast(U32), axis=0),
                                                    in_=DT[:, t, k, :], in_offset=None).then_inc(s_tab[i], 16)

            pool.wait_ge(s_plan, 1)
            quads = pool.value_load(NQI[0:1, 0:1], min_val=LEAST, max_val=MAXT // CHAINS)
            past, now, ahead = (pool.alloc_register(f"bodies_{i}") for i in ("past", "now", "ahead"))
            for register, value in ((past, 0), (now, 1), (ahead, 2)):
                pool.reg_mov(register, value)
            pool.wait_ge(s_rd, 16 * B)
            pool.wait_ge(s_zs, 16 * CHAINS)

            def gather(i):
                pool.indirect_dma_start(out=XR[:, i, :], out_offset=None, in_=rows_dram,
                                        in_offset=bass.IndirectOffsetOnAxis(ap=IG[:, i:i + 1].bitcast(U32), axis=0),
                                        bounds_check=TOK - 1, oob_is_err=False).then_inc(s_xr[i], 16)

            def add(i):
                pool.indirect_dma_start(out=sums_dram[i], out_offset=bass.IndirectOffsetOnAxis(ap=IS[:, i:i + 1].bitcast(U32), axis=0),
                                        in_=OB[:, i, :], in_offset=None, bounds_check=TOK - 1, oob_is_err=False,
                                        compute_op=ALU.add).then_inc(s_add[i], 16)

            for i in range(CHAINS):
                pool.wait_ge(s_ig[i], 1)
                gather(i)
            for i in range(CHAINS):
                pool.wait_ge(s_ig[i], 2)
                pool.wait_ge(s_et[i], 1)
                gather(i)
                if i >= 2:
                    pool.wait_ge(s_ob[i - 2], 1)
                    add(i - 2)
            with pool.Fori(1, quads):
                for register in (past, now, ahead):
                    pool.reg_add(register, register, 1)
                for i in range(CHAINS):
                    pool.wait_ge(s_lc, 64)
                    pool.wait_ge(s_ig[i], ahead)
                    pool.wait_ge(s_et[i], now)
                    gather(i)
                    j = (i - 2) % CHAINS
                    pool.wait_ge(s_lc, 64)
                    pool.wait_ge(s_ob[j], now if i >= 2 else past)
                    add(j)
            for i in range(2, CHAINS):
                pool.wait_ge(s_lc, 64)
                pool.wait_ge(s_ob[i], quads)
                add(i)
            for i in range(CHAINS):
                pool.wait_ge(s_xr[i], quads * 16 + 16)

        @block.scalar
        def _(act):
            act.wait_ge(s_pool0, 8)

            for n in SLOTS:
                if 0 <= n < B * H:
                    act.wait_ge(s_tr, (n + 1) * 2)
                    if n >= 2:
                        act.wait_ge(s_pp, n - 1)
                    for c, (lo, hi) in enumerate(((0, P), (P, SC))):
                        act.activation(PR[:, n % 2, lo:hi], ps[:, n % 2, lo:hi], ACT.Exp, bias=MN[:, n % 4, c:c + 1], scale=-1.0).then_inc(s_ex, 1)
                for p, name in steps(n):
                    if name in TURNS:
                        act.wait_ge(s_tp, TURN_NO[p, name] + 1)
                        act.activation(XT[:, TURNS.index(name), :, :], ps[:, 5, :].rearrange("p (k s) -> p k s", k=KD), ACT.Copy).then_inc(s_xt, 1)
                    if name in ("q0", "q1"):
                        bank, used = produced(act, p, name)
                        for c in range(2):
                            g = int(name[1]) * 2 + c
                            last = act.activation(QT[:, p % 2, g, :], ps[:, bank, c * S:(c + 1) * S], ACT.Identity,
                                                  bias=BQN[:, g:g + 1], scale=-(HD ** -0.5))
                        last.then_inc(used, 1)
                    if name in ("z01", "z11"):
                        t = int(name[1])
                        consumed(act, p, name)
                        if p:
                            act.wait_ge(s_ag, (p - 1) * TB + t + 1)
                        act.activation(TH[:, t, :], Z[:, t, :], ACT.Tanh, scale=0.5).then_inc(s_th, 1)
                    if name == "top":
                        bank, used = produced(act, p, "lg")
                        act.wait_ge(s_nm, p + 1)
                        if p:
                            act.wait_ge(s_pb, p * TB)
                        for t in range(TB):
                            last = act.activation(EL[:, t, :], ps[:, bank, t * E:(t + 1) * E], ACT.Exp, bias=NM[:, t:t + 1],
                                                  accum_out=SE[:, t:t + 1])
                        last.then_inc(used, 1)

            act.wait_ge(s_plan, 1)
            quads = act.value_load(NQI[0:1, 0:1], min_val=LEAST, max_val=MAXT // CHAINS)

            def gate(q, i):
                act.wait_ge(s_gu[i], q + 1)
                act.activation(SG[:, i, :], ps[:, 2 + i % 2, 0:P], ACT.Silu).then_inc(s_sg[i], 1)

            def rows_weighted(q, i, first=False):
                act.wait_ge(s_o[i], q + 1)
                if not first:
                    act.wait_ge(s_add[i], q * 16)
                act.activation(IS[:, i:i + 1], IW[:, bass.ds(q * CHAINS + i, 1), 0], ACT.Copy)
                act.activation(OB[:, i, :], ps[:, 4 + i % 2, 0:D], ACT.Copy,
                               scale=IW[:, bass.ds(q * CHAINS + i, 1), 1]).then_inc(s_ob[i], 1)

            def body(q, first=False):
                for i in range(CHAINS):
                    gate(q, i)
                    if i:
                        rows_weighted(q, i - 1, first)
                rows_weighted(q, CHAINS - 1, first)

            body(0, first=True)
            with act.Fori(1, quads) as q:
                body(q)

        @block.tensor
        def _(pe):
            pe.wait_ge(s_lc, 64)

            def turn(p, name):
                if name == "t_ao":
                    pe.wait_ge(s_ao, (p + 1) * 2)
                    rows_of = lambda t, k: AO[:, t, k * 8:(k + 1) * 8, :].rearrange("p h d -> p (h d)")
                elif name == "t_a":
                    pe.wait_ge(s_aa, (p + 1) * TB)
                    rows_of = lambda t, k: AA[:, t, k * P:(k + 1) * P]
                else:
                    n = ("t_x", "t_x2", "t_x3").index(name)
                    pe.wait_ge(s_xn, (LN_NO[p, f"ln{n + 1}"] + 1) * TB)
                    rows_of = lambda t, k: XN[:, n, t, k * P:(k + 1) * P]
                if TURN_NO[p, name]:
                    pe.wait_ge(s_xt, TURN_NO[p, name])
                for t in range(TB):
                    for k in range(KD):
                        last = pe.transpose(ps[:, 5, k * S + t * P:k * S + (t + 1) * P], rows_of(t, k), ident)
                last.then_inc(s_tp, 1)

            def unit(p, name):
                n = UNIT_NO[p, name]
                bank = 6 + n % 2
                if n >= 2:
                    pe.wait_ge(s_used[n % 2], n // 2)
                source = {"q": "t_x", "k": "t_x", "v": "t_x", "w": "t_ao", "z": "t_x2", "y": "t_a", "l": "t_x3"}.get(name[0])
                if source:
                    pe.wait_ge(s_xt, TURN_NO[p, source] + 1)
                    xt = XT[:, TURNS.index(source), :, :]
                if name[0] in "qk":
                    pe.wait_ge(s_lw, 16)
                    for c in range(2):
                        g = int(name[1]) * 2 + c
                        for k in range(KD):
                            last = pe.matmul(ps[:, bank, c * S:(c + 1) * S], WQK[:, k, "qk".index(name[0]), g * P:(g + 1) * P],
                                             xt[:, k, :], start=(k == 0), stop=(k == KD - 1))
                elif name[0] in "zy":
                    pe.wait_ge(s_lct, 32)
                    t, half = int(name[1]), int(name[2])
                    for k in range(KD):
                        last = pe.matmul(ps[:, bank, :], xt[:, k, t * P:(t + 1) * P], CT[:, k, half * 512:(half + 1) * 512],
                                         start=(k == 0), stop=(k == KD - 1))
                elif name == "cum":
                    pe.wait_ge(s_sel, (p + 1) * TB)
                    if p:
                        pe.wait_ge(s_cnt, p * TB)
                    for t in range(TB):
                        o = ps[:, bank, t * E:(t + 1) * E]
                        pe.matmul(o, TRI[:, :], SELB[:, t, :], start=True, stop=False)
                        if t == 1:
                            pe.matmul(o, ONES[:, :], SELB[:, 0, :], start=False, stop=False)
                        last = pe.matmul(o, ONES[:, :], CNT[:, :], start=False, stop=True)
                else:
                    loaded, needed, weights, width = {"v": (s_lwv, 16, WV, D), "wo": (s_lwo, 16, WO, D), "lg": (s_lct, 32, GT, E)}[name]
                    pe.wait_ge(loaded, needed)
                    for t in range(TB):
                        for k in range(KD):
                            last = pe.matmul(ps[:, bank, t * width:(t + 1) * width], xt[:, k, t * P:(t + 1) * P], weights[:, k, :],
                                             start=(k == 0), stop=(k == KD - 1))
                last.then_inc(s_unit[n % 2], 1)

            for n in SLOTS:
                if 0 <= n < B * H:
                    p, h = divmod(n, H)
                    if h % 8 == 0:
                        consumed(pe, p, f"q{h // 8}")
                        consumed(pe, p, f"k{h // 8}")
                    if n >= 2:
                        pe.wait_ge(s_ex, (n - 1) * 2)
                    g, lo = h // GH, (h % GH) * SLOT
                    q, k = QT[lo:lo + SLOT, p % 2, g, :], KT[lo:lo + SLOT, p % 2, g, :]
                    pe.matmul(ps[:, n % 2, 0:P], q[:, 0:P], k[:, 0:P], start=True, stop=True, tile_position=(lo, 0))
                    pe.matmul(ps[:, n % 2, P:SC], q[:, P:S], k[:, 0:S], start=True, stop=True, tile_position=(lo, 0)).then_inc(s_sc, 1)
                j = n - 2
                if 0 <= j < B * H:
                    pe.wait_ge(s_ex, (j + 1) * 2)
                    if j >= 2:
                        pe.wait_ge(s_pt, j - 1)
                    for c in range(3):
                        last = pe.transpose(ps[:, 2 + j % 2, c * P:(c + 1) * P], PR[:, j % 2, c * P:(c + 1) * P], ident)
                    last.then_inc(s_pp, 1)
                j = n - 3
                if 0 <= j < B * H:
                    p, h = divmod(j, H)
                    if h == 0:
                        consumed(pe, p, "v")
                    if h % 8 == 0 and j:
                        pe.wait_ge(s_ao, j // 8)
                    pe.wait_ge(s_pt, j + 1)
                    o0, o1 = (ps[:, 4, (t * 8 + h % 8) * HV:(t * 8 + h % 8 + 1) * HV] for t in range(TB))
                    pe.matmul(o0, PT[:, j % 2, 0:P], VA[:, p % 2, 0, h, :], start=True, stop=True)
                    pe.matmul(o1, PT[:, j % 2, P:2 * P], VA[:, p % 2, 0, h, :], start=True, stop=False)
                    pe.matmul(o1, PT[:, j % 2, 2 * P:3 * P], VA[:, p % 2, 1, h, :], start=False, stop=True).then_inc(s_pv, 1)
                for p, name in steps(n):
                    if name in TURNS:
                        turn(p, name)
                    if name in UNITS:
                        unit(p, name)

            pe.wait_ge(s_cnt, B * TB)
            pe.matmul(ps[0:E, 0, 0:1], CNT[:, :], ONES[:, 0:1], start=True, stop=True).then_inc(s_cn, 1)
            pe.wait_ge(s_ni, 3)
            pe.matmul(ps[0:E, 0, 1:2], TRI[0:E, 0:E], NBF[:, :], start=True, stop=True)
            pe.matmul(ps[:, 0, 2:3], ONES[0:E, :], NBF[:, :], start=True, stop=True).then_inc(s_cn, 1)
            pe.wait_ge(s_m, 3)
            pe.matmul(ps[:, 1, 0:P], ONEF[0:E, :], M1[:, :], start=True, stop=True).then_inc(s_cn, 1)
            pe.wait_ge(s_oh, NQ)
            pe.wait_ge(s_lt, 16 * CHAINS)
            for c in range(2):
                for i in range(CHAINS):
                    for n in range(NQ):
                        last = pe.matmul(ps[:, 2, c * P:(c + 1) * P], TABLE[:, i, n, :].rearrange("p (s c) -> p s c", c=2)[:, :, c],
                                         OH[:, n, :], start=(i == 0 and n == 0), stop=(i == CHAINS - 1 and n == NQ - 1))
            last.then_inc(s_cn, 1)

            pe.wait_ge(s_plan, 1)
            quads = pe.value_load(NQI[0:1, 0:1], min_val=LEAST, max_val=MAXT // CHAINS)

            def rows_turned(q, i):
                for k in range(KD):
                    last = pe.transpose(ps[:, i % 2, k * P:(k + 1) * P], XR[:, i, k * P:(k + 1) * P], ident)
                last.then_inc(s_et[i], 1)

            def up(q, i, first=False):
                pe.wait_ge(s_w[i], q * 32 + 32)
                pe.wait_ge(s_ext[i], q + 1)
                if i >= 2:
                    pe.wait_ge(s_h[i - 2], q + 1)
                elif not first:
                    pe.wait_ge(s_h[i + 2], q)
                for c in range(2):
                    for k in range(KD):
                        last = pe.matmul(ps[:, 2 + i % 2, c * P:(c + 1) * P], W13[:, i, k, c * F:(c + 1) * F], XRT[:, i, k, :],
                                         start=(k == 0), stop=(k == KD - 1))
                last.then_inc(s_gu[i], 1)

            def down(i):
                pe.matmul(ps[:, 4 + i % 2, 0:D], HT[:, i, :], W2[:, i, :], start=True, stop=True).then_inc(s_o[i], 1)

            def body(q, first=False):
                for i in range(CHAINS):
                    if i < CHAINS - 1:
                        pe.wait_ge(s_xr[i + 1], q * 16 + 16)
                    else:
                        pe.wait_ge(s_xr[0], q * 16 + 32)
                    if i:
                        pe.wait_ge(s_ext[i - 1], q + 1)
                    elif not first:
                        pe.wait_ge(s_ext[CHAINS - 1], q)
                    rows_turned(q, (i + 1) % CHAINS)
                    up(q, i, first)
                    if i:
                        pe.wait_ge(s_h[i - 1], q + 1)
                        if i == CHAINS - 1:
                            pe.wait_ge(s_ob[0], q + 1)
                        elif not first:
                            pe.wait_ge(s_ob[i + 1], q)
                        down(i - 1)
                    elif not first:
                        pe.wait_ge(s_h[CHAINS - 1], q)
                        pe.wait_ge(s_ob[1], q)
                        down(CHAINS - 1)

            pe.wait_ge(s_xr[0], 16)
            rows_turned(0, 0)
            body(0, first=True)
            with pe.Fori(1, quads) as q:
                body(q)
            pe.wait_ge(s_h[CHAINS - 1], quads)
            pe.wait_ge(s_ob[1], quads)
            down(CHAINS - 1)

        @block.vector
        def _(dve):
            dve.wait_ge(s_lc, 64)
            for n in range(3):
                dve.tensor_scalar(GE[:, n, :], TID[:, :], float(THIRD * (n + 1)), None, ALU.is_ge).then_inc(s_ge, 1)
            dve.wait_ge(s_ge, 3)
            dve.tensor_scalar(MSK[:, :, 0], GE[:, 0, :], -1.0, 1.0, ALU.mult, ALU.add).then_inc(s_ge, 1)
            dve.tensor_tensor(MSK[:, :, 1], GE[:, 0, :], GE[:, 1, :], ALU.subtract).then_inc(s_ge, 1)
            dve.tensor_tensor(MSK[:, :, 2], GE[:, 1, :], GE[:, 2, :], ALU.subtract).then_inc(s_ge, 1)
            dve.tensor_copy(MSK[:, :, 3], GE[:, 2, :]).then_inc(s_ge, 1)
            dve.wait_ge(s_ge, 7)
            dve.wait_ge(s_pool0, 8)
            dve.wait_ge(s_lx, 16)

            def source(p, t, name):
                return X2[:, t, :] if name[-1] == "2" else (X if name[-1] == "1" else X3)[:, p * TB + t, :]

            def mask(p, t, e):
                return MSK[:, p * TB + t, e:e + 1]

            def step(p, name):
                if name in ("ln1", "ln2", "ln3"):
                    k = LN_NO[p, name]
                    n = int(name[2]) - 1
                    if p:
                        dve.wait_ge(s_xn, (LN_NO[p - 1, name] + 1) * TB)
                    if name == "ln2":
                        consumed(dve, p, "wo")
                    if name == "ln3":
                        consumed(dve, p, "y01")
                        consumed(dve, p, "y11")
                    for t in range(TB):
                        dve.bn_stats(ST[:, n, t, :], source(p, t, name)).then_inc(s_st, 1)
                    for t in range(TB):
                        dve.wait_ge(s_st, k * TB + t + 1)
                        dve.bn_aggr(MV[:, n, t, :], ST[:, n, t, :]).then_inc(s_mv, 1)
                if name in ("n1", "n2", "n3"):
                    n = int(name[1])
                    dve.wait_ge(s_rstd, LN_NO[p, f"ln{n}"] + 1)
                    if p:
                        dve.wait_ge(s_tp, TURN_NO[p - 1, ("t_x", "t_x2", "t_x3")[n - 1]] + 1)
                    if p and n == 3:
                        dve.wait_ge(s_rd, p * 16)
                    for t in range(TB):
                        dve.tensor_scalar(XN[:, n - 1, t, :], source(p, t, name), MV[:, n - 1, t, 0:1], RSTD[:, n - 1, t:t + 1],
                                          ALU.subtract, ALU.mult).then_inc(s_xn, 1)
                if name in ("k0", "k1"):
                    bank, used = produced(dve, p, name)
                    for c in range(2):
                        g = int(name[1]) * 2 + c
                        last = dve.tensor_scalar(KT[:, p % 2, g, :], ps[:, bank, c * S:(c + 1) * S], BQK[:, 1, g:g + 1], None, ALU.add)
                    last.then_inc(used, 1)
                if name == "v":
                    bank, used = produced(dve, p, name)
                    for t in range(TB):
                        last = dve.tensor_tensor(VA[:, p % 2, t, :, 0:HD], ps[:, bank, t * D:(t + 1) * D].rearrange("p (h d) -> p h d", h=H),
                                                 BROW[:, 0, :].rearrange("p (h d) -> p h d", h=H), ALU.add)
                    last.then_inc(used, 1)
                if name == "wo":
                    bank, used = produced(dve, p, name)
                    dve.wait_ge(s_xb, NT)
                    for t in range(TB):
                        last = dve.tensor_tensor(X2[:, t, :], ps[:, bank, t * D:(t + 1) * D], XB[:, p * TB + t, :], ALU.add)
                    last.then_inc(used, 1)
                if name[0] == "z":
                    bank, used = produced(dve, p, name)
                    t, half = int(name[1]), int(name[2])
                    if half == 0:
                        if p:
                            dve.wait_ge(s_aa, (p - 1) * TB + t + 1)
                        dve.tensor_scalar(Z[:, t, :], ps[:, bank, 0:D], mask(p, t, 0), None, ALU.mult).then_inc(s_z, 1)
                    else:
                        consumed(dve, p, f"z{t}0")
                        dve.scalar_tensor_tensor(Z[:, t, :], ps[:, bank, 0:D], mask(p, t, 2), Z[:, t, :], ALU.mult, ALU.add).then_inc(s_z, 1)
                    dve.wait_ge(s_z, (p * TB + t) * 2 + half + 1)
                    dve.scalar_tensor_tensor(Z[:, t, :], ps[:, bank, D:2 * D], mask(p, t, half * 2 + 1), Z[:, t, :],
                                             ALU.mult, ALU.add).then_inc(used, 1)
                if name in ("a0", "a1"):
                    t = int(name[1])
                    dve.wait_ge(s_th, p * TB + t + 1)
                    if p:
                        dve.wait_ge(s_tp, TURN_NO[p - 1, "t_a"] + 1)
                    dve.scalar_tensor_tensor(AA[:, t, :], TH[:, t, :], 1.0, Z[:, t, :], ALU.add, ALU.mult).then_inc(s_ag, 1)
                    dve.wait_ge(s_ag, p * TB + t + 1)
                    dve.scalar_tensor_tensor(AA[:, t, :], AA[:, t, :], 0.5, Z[:, t, :], ALU.mult, ALU.mult).then_inc(s_aa, 1)
                if name[0] == "y":
                    bank, used = produced(dve, p, name)
                    t, half = int(name[1]), int(name[2])
                    x3 = X3[:, p * TB + t, :]
                    if half:
                        consumed(dve, p, f"y{t}0")
                    dve.scalar_tensor_tensor(x3, ps[:, bank, 0:D], mask(p, t, half * 2), x3 if half else X2[:, t, :],
                                             ALU.mult, ALU.add).then_inc(s_y, 1)
                    dve.wait_ge(s_y, (p * TB + t) * 2 + half + 1)
                    dve.scalar_tensor_tensor(x3, ps[:, bank, D:2 * D], mask(p, t, half * 2 + 1), x3, ALU.mult, ALU.add).then_inc(used, 1)
                if name == "top":
                    bank, used = produced(dve, p, "lg")
                    for t in range(TB):
                        dve.max(ML[:, t, :], ps[:, bank, t * E:(t + 1) * E]).then_inc(s_ml, 1)
                    dve.wait_ge(s_ml, (p + 1) * TB)
                    dve.tensor_scalar(NM[:, :], ML[:, :, 0], -1.0, None, ALU.mult).then_inc(s_nm, 1)
                if name == "pick":
                    consumed(dve, p, "lg")
                    dve.reciprocal(RE[:, :], SE[:, :]).then_inc(s_re, 1)
                    dve.wait_ge(s_re, p + 1)
                    for t in range(TB):
                        dve.tensor_scalar(PB[:, t, :], EL[:, t, :], RE[:, t:t + 1], None, ALU.mult).then_inc(s_pb, 1)
                    for t in range(TB):
                        dve.wait_ge(s_pb, p * TB + t + 1)
                        dve.max(M8[:, t, :], PB[:, t, :]).then_inc(s_m8, 1)
                    for t in range(TB):
                        dve.wait_ge(s_m8, p * TB + t + 1)
                        dve.match_replace(PX[:, t, :], M8[:, t, :], PB[:, t, :], -1.0).then_inc(s_px, 1)
                    for t in range(TB):
                        dve.wait_ge(s_px, p * TB + t + 1)
                        dve.tensor_scalar(SELB[:, t, :], PX[:, t, :], 0.0, None, ALU.is_lt).then_inc(s_sel, 1)
                    for t in range(TB):
                        dve.tensor_scalar(SEL[:, t, :], PX[:, t, :], 0.0, None, ALU.is_lt).then_inc(s_eq, 1)
                    dve.wait_ge(s_eq, p * 4 + 2)
                    dve.tensor_tensor(CW[:, :, :], PB[:, :, :], SEL[:, :, :], ALU.mult).then_inc(s_cw, 1)
                if name == "slot":
                    bank, used = produced(dve, p, "cum")
                    for t in range(TB):
                        if p or t:
                            dve.wait_ge(s_cnt, p * TB + t)
                        dve.tensor_tensor(CNT[:, :], CNT[:, :], SELB[:, t, :], ALU.add).then_inc(s_cnt, 1)
                    for t in range(TB):
                        dve.tensor_tensor(SV[:, t, :], ps[:, bank, t * E:(t + 1) * E], C[:, C_SLOT:C_SLOT + E],
                                          ALU.add).then_inc(used if t else s_sv, 1)
                    dve.wait_ge(s_sv, p * 2 + 1)
                    consumed(dve, p, "cum")
                    dve.tensor_tensor(SV[:, :, :], SV[:, :, :], SEL[:, :, :], ALU.mult).then_inc(s_sv, 1)
                    dve.wait_ge(s_sv, p * 2 + 2)
                    for t in range(TB):
                        dve.max(V8[:, t, :], SV[:, t, :]).then_inc(s_v8, 1)
                    dve.wait_ge(s_v8, (p + 1) * TB)
                    if p:
                        for i in range(CHAINS):
                            dve.wait_ge(s_tab[i], p * 16 * (TB * TOPK // CHAINS))
                    dve.tensor_scalar(IX[:, :, :], V8[:, :, :], -1.0, None, ALU.add).then_inc(s_dt, 1)
                    dve.tensor_tensor(EQ[:, :, :, :], V8[:, :, :].unsqueeze(3).to_broadcast([P, TB, TOPK, E]),
                                      SV[:, :, :].unsqueeze(2).to_broadcast([P, TB, TOPK, E]), ALU.is_equal).then_inc(s_eq, 1)
                    dve.wait_ge(s_eq, p * 4 + 3)
                    dve.wait_ge(s_cw, p + 1)
                    dve.tensor_tensor(EQ[:, :, :, :], EQ[:, :, :, :], CW[:, :, :].unsqueeze(2).to_broadcast([P, TB, TOPK, E]), ALU.mult).then_inc(s_eq, 1)
                    dve.tensor_copy(DT[:, :, :, 0], C[:, p * TB + C_TOK:(p + 1) * TB + C_TOK].unsqueeze(2).to_broadcast([P, TB, TOPK])).then_inc(s_dt, 1)
                    dve.wait_ge(s_eq, p * 4 + 4)
                    dve.tensor_reduce(DT[:, :, :, 1], EQ[:, :, :, :], AX_X, ALU.add).then_inc(s_dt, 1)

            for n in SLOTS:
                if n == 0:
                    dve.wait_ge(s_lnb, 16)
                if 0 <= n < B * H:
                    dve.wait_ge(s_sc, n + 1)
                    for c, (lo, hi) in enumerate(((0, P), (P, SC))):
                        dve.tensor_tensor_reduce(ps[:, n % 2, lo:hi], ps[:, n % 2, lo:hi], NB[:, n % H, lo:hi], 1.0, 3e38, ALU.add, ALU.min,
                                                 MN[:, n % 4, c:c + 1]).then_inc(s_tr, 1)
                for p, name in steps(n):
                    if name in ("n1", "n2", "n3"):
                        step(p, name)
                j = n - 2
                if 0 <= j < B * H:
                    dve.wait_ge(s_pp, j + 1)
                    if j >= 2:
                        dve.wait_ge(s_pv, j - 1)
                    dve.tensor_copy(PT[:, j % 2, :], ps[:, 2 + j % 2, 0:SC]).then_inc(s_pt, 1)
                j = n - 4
                if 0 <= j < B * H and j % 8 == 7:
                    p, half = divmod(j // 8, 2)
                    o = ps[:, 4, 0:TB * 8 * HV].rearrange("p (t h d) -> p t h d", t=TB, h=8)
                    dve.wait_ge(s_pv, j + 1)
                    dve.reciprocal(RS[:, :, half * 8:half * 8 + 8], o[:, :, :, HD]).then_inc(s_rs, 1)
                    dve.wait_ge(s_rs, j // 8 + 1)
                    if p:
                        dve.wait_ge(s_tp, TURN_NO[p - 1, "t_ao"] + 1)
                    dve.tensor_tensor(AO[:, :, half * 8:half * 8 + 8, :], o[:, :, :, 0:HD],
                                      RS[:, :, half * 8:half * 8 + 8].unsqueeze(3).to_broadcast([P, TB, 8, HD]), ALU.mult).then_inc(s_ao, 1)
                for p, name in steps(n):
                    if name not in ("n1", "n2", "n3"):
                        step(p, name)

            dve.wait_ge(s_cn, 1)
            dve.tensor_scalar(NI[:, 0:1], ps[0:E, 0, 0:1], float(P - 1), None, ALU.add).then_inc(s_ni, 1)
            dve.wait_ge(s_ni, 1)
            dve.tensor_scalar(NI[:, 1:2], NI[:, 0:1], 7, None, ALU.logical_shift_right).then_inc(s_ni, 1)
            dve.wait_ge(s_ni, 2)
            dve.tensor_copy(NBF[:, :], NI[:, 1:2]).then_inc(s_ni, 1)
            dve.wait_ge(s_cn, 2)
            dve.tensor_copy(SN[:, 0:1], ps[0:E, 0, 1:2]).then_inc(s_stt, 1)
            dve.tensor_copy(NTF[:, :], ps[:, 0, 2:3]).then_inc(s_stt, 1)
            dve.wait_ge(s_ni, 3)
            dve.tensor_tensor(SN[:, 1:2], ps[0:E, 0, 1:2], NBF[:, :], ALU.add).then_inc(s_stt, 1)
            dve.tensor_tensor(SN[:, 2:3], C[0:E, C_E8:C_E8 + 1], ps[0:E, 0, 1:2], ALU.subtract).then_inc(s_stt, 1)
            dve.wait_ge(s_stt, 4)
            dve.tensor_scalar(M1[:, :], C[0:E, C_IOTA:C_IOTA + P], SN[:, 2:3], None, ALU.add).then_inc(s_m, 1)
            dve.wait_ge(s_m, 1)
            dve.scalar_tensor_tensor(M2[:, :], C[0:E, C_IOTA:C_IOTA + P], SN[:, 0:1], M1[:, :], ALU.is_ge, ALU.mult).then_inc(s_m, 1)
            dve.wait_ge(s_m, 2)
            dve.scalar_tensor_tensor(M1[:, :], C[0:E, C_IOTA:C_IOTA + P], SN[:, 1:2], M2[:, :], ALU.is_lt, ALU.mult).then_inc(s_m, 1)
            dve.tensor_scalar(LATE[:, :], iota, NTF[:, 0:1], 8.0 * TOK, ALU.is_ge, ALU.mult).then_inc(s_cb, 1)
            dve.tensor_scalar(NQI[0:1, 1:2], NTF[0:1, :], float(CHAINS - 1), None, ALU.add).then_inc(s_cb, 1)
            dve.wait_ge(s_cn, 3)
            dve.wait_ge(s_cb, 2)
            dve.tensor_tensor(CB[:, :], LATE[:, :], ps[:, 1, 0:P], ALU.add).then_inc(s_cb, 1)
            dve.tensor_scalar(NQI[0:1, 0:1], NQI[0:1, 1:2], 2, None, ALU.logical_shift_right).then_inc(s_cb, 1)
            dve.wait_ge(s_cb, 4)
            for n in range(NQ):
                dve.tensor_scalar(OH[:, n, :], CB[:, :], C[:, C_PQ + n:C_PQ + n + 1], None, ALU.is_equal).then_inc(s_oh, 1)
            dve.tensor_scalar(EJ[:, 1, :], CB[0:1, :], 8.0 * E - 1, None, ALU.min).then_inc(s_cb, 1)
            dve.wait_ge(s_cb, 5)
            dve.tensor_scalar(EJ[:, 0, :], EJ[:, 1, :], 3, None, ALU.logical_shift_right).then_inc(s_cb, 1)
            dve.wait_ge(s_cb, 6)
            dve.memset(IW[:, MAXT:MAXT + CHAINS, :], float(EMPTY)).then_inc(s_iw, 1)
            dve.wait_ge(s_cn, 4)
            dve.tensor_scalar(IW[:, 0:MAXT, 0], ps[:, 2, 0:P], float(EMPTY), None, ALU.add).then_inc(s_iw, 1)
            dve.tensor_copy(IW[:, 0:MAXT, 1], ps[:, 2, P:2 * P]).then_inc(s_iw, 1)
            dve.wait_ge(s_iw, 3)
            for i in range(CHAINS):
                dve.tensor_copy(IG[:, i:i + 1], IW[:, i, 0:1]).then_inc(s_ig[i], 1)
            dve.engine_nop().then_inc(s_plan, 1)

            quads = dve.value_load(NQI[0:1, 0:1], min_val=LEAST, max_val=MAXT // CHAINS)

            def rows_out(q, i):
                dve.wait_ge(s_et[i], q + 1)
                dve.tensor_copy(XRT[:, i, :, :], ps[:, i % 2, 0:KD * P].rearrange("p (k s) -> p k s", k=KD)).then_inc(s_ext[i], 1)

            def body(q):
                for i in range(CHAINS):
                    rows_out(q if i < CHAINS - 1 else q + 1, (i + 1) % CHAINS)
                    dve.wait_ge(s_xr[i], q * 16 + 16)
                    dve.tensor_copy(IG[:, i:i + 1], IW[:, bass.ds(q * CHAINS + CHAINS + i, 1), 0]).then_inc(s_ig[i], 1)
                    dve.wait_ge(s_sg[i], q + 1)
                    dve.tensor_tensor(HT[:, i, :], ps[:, 2 + i % 2, P:2 * P], SG[:, i, :], ALU.mult).then_inc(s_h[i], 1)

            rows_out(0, 0)
            body(0)
            with dve.Fori(1, quads) as q:
                body(q)

            x3 = X3[:, :, :].rearrange("p n d -> p (n d)")
            for i in range(CHAINS):
                dve.wait_ge(s_fl[i], 16)
                if i:
                    dve.wait_ge(s_fs, i)
                dve.tensor_tensor(x3, x3, sums[i], ALU.add).then_inc(s_fin if i == CHAINS - 1 else s_fs, 1)


def _consts():
    import numpy as np

    c = np.zeros((P, C_W), np.float32)
    p, j = np.arange(P)[:, None], np.arange(P)[None, :]
    c[:, C_ID:C_ID + P] = p == j
    c[:, C_TRI:C_TRI + P] = p < j
    c[:, C_IOTA:C_IOTA + P] = j
    c[:, C_PQ:C_PQ + NQ] = p + P * np.arange(NQ)
    c[:, C_SLOT:C_SLOT + E] = CAP * np.arange(E) + 1
    c[:, C_TOK:C_TOK + NT] = p + P * np.arange(NT) - EMPTY
    c[:, C_E8] = CAP // P * np.arange(P)
    start = 2 ** (-2 ** (-(np.log2(H) - 3)))
    slopes = np.array([start * start ** i for i in range(H)], np.float32)
    key = np.concatenate([np.arange(P), np.arange(S)])
    query = np.arange(P)[:, None] + np.where(np.arange(SC) < P, 0, P)
    nb = slopes[None, :, None] * (S - 1 - key).astype(np.float32)[None, None, :]
    nb = np.where((key[None, :] > query)[:, None, :], np.float32(1e37), nb).astype(np.float32)
    return c, nb


def kernel(x, itok_BxS_13_99985, ctx_2048, L0_attn_Wq, L0_attn_bq, L0_attn_Wk, L0_attn_bk, L0_attn_Wv, L0_attn_bv,
           L0_attn_Wo, L0_attn_bo, L0_ffn_gate_w, L0_ffn_w13, L0_ffn_w2):
    import numpy as np
    import concourse.bacc as bacc
    from concourse.bass_utils import run_bass_kernel_spmd

    def slots(w, bias=False):
        w = np.asarray(w).reshape(-1, H, HD)
        out = np.zeros((w.shape[0], H, SLOT), np.float32)
        out[:, :, :HD] = w
        return out.reshape(-1, H * SLOT)

    def slot_rows(v):
        return slots(v).reshape(NG, P).T

    consts, neg_bias = _consts()
    arrays = {
        "x": np.asarray(x).reshape(TOK, D),
        "tok_ids": np.asarray(itok_BxS_13_99985).reshape(NT, P).T,
        "ctx_t": np.asarray(ctx_2048).transpose(2, 0, 1).reshape(D, EX * CTX),
        "wqk": np.stack([slots(L0_attn_Wq), slots(L0_attn_Wk)], axis=1),
        "wv": np.asarray(L0_attn_Wv),
        "wo": np.asarray(L0_attn_Wo),
        "bqk": np.stack([slot_rows(L0_attn_bq), slot_rows(L0_attn_bk)], axis=1),
        "rows": np.stack([np.asarray(L0_attn_bv), np.asarray(L0_attn_bo)]),
        "gate_t": np.asarray(L0_ffn_gate_w).T,
        "w13_t": np.asarray(L0_ffn_w13).transpose(0, 2, 1),
        "w2_t": np.asarray(L0_ffn_w2).transpose(0, 2, 1),
        "consts": consts,
        "neg_bias": neg_bias,
    }
    arrays = {k: np.ascontiguousarray(v) for k, v in arrays.items()}
    nc = bacc.Bacc("TRN2", target_bir_lowering=False, num_devices=1)
    args = [nc.dram_tensor(f"in_{k}", v.shape, mybir.dt.from_np(v.dtype), kind="ExternalInput").ap() for k, v in arrays.items()]
    out = nc.dram_tensor("out", (TOK, D), F32, kind="ExternalOutput").ap()
    decoder_kernel(nc, *args, out)
    r = run_bass_kernel_spmd(nc, [{f"in_{k}": v for k, v in arrays.items()}], core_ids=[0])
    return r.results[0]["out"].reshape(B, S, D)
```

```python
from contextlib import ExitStack

import concourse.bass as bass
from concourse import mybir

ALU = mybir.AluOpType
ACT = mybir.ActivationFunctionType
F32 = mybir.dt.float32
BF16 = mybir.dt.bfloat16
F32R = mybir.dt.float32r
I32 = mybir.dt.int32
U32 = mybir.dt.uint32
AX_X = mybir.AxisListType.X

P = 128
B, S, D = 4, 256, 256
TOK = B * S
NT = TOK // P
TB = S // P
KD = D // P
H, HD = 16, 16
SLOT = 32
PAIR = SLOT // HD
NG = D // P
HG = H // NG
GO = P // SLOT
SC = P + S
EX, CTX = 4, 256
THIRD = 12500 // EX
E, TOPK, F = 64, 8, 128
CAP = TOK
COLS = E * CAP // P
CHAINS = 4
LEAST = TOK * TOPK // P // CHAINS
MAXT = 128
EMPTY = 4096
EPS = 1e-5

PARTS = 2
def of_tiles(**first):
    return {f"{kind}_{t}": slot + 2 * t for t in range(TB) for kind, slot in first.items()}


AT = of_tiles(ln1=-21, n1=-20) | {"tx": -17, "q": -14, "k": -12, "v": -3, "to0": 7, "to1": 11, "to2": 15, "to3": 19} | of_tiles(
    tao=20, wo=21, ln2=21, n2=22, tx2=23, za=24, zb=25, a=26, ta=27, ya=28, yb=29, ln3=29, n3=30, tx3=31, lg=32, top=32, pick=33,
    cum=34, slot=34, same=35, weigh=36, pairs=36, scatter=38)
SLOTS = range(min(AT.values()), (B - 1) * H + max(AT.values()) + PARTS)
ROWS = ("tx", "tao", "tx2", "ta", "tx3")
SPLIT = ("tx2", "ta")
OUTS = ("to0", "to1", "to2", "to3")
TURNS = ROWS + OUTS
UNITS = ("q", "k", "v", "wo", "za", "zb", "ya", "yb", "lg", "cum")
NORMS = ("ln1", "ln2", "ln3")


def kind(name):
    return name.split("_")[0]


def steps(n):
    return [(p, name, int(name[-1]) if "_" in name else 0) for p in range(B) for name in AT if n - p * H == AT[name]]


def numbered(kinds):
    order = [(p, name) for n in SLOTS for p, name, t in steps(n) if kind(name) in kinds]
    return {key: i for i, key in enumerate(order)}


TURN_NO = numbered(TURNS)
UNIT_NO = numbered(UNITS)
LN_NO = numbered(NORMS)
XS_NO = numbered(SPLIT)


C_ID, C_TRI, C_IOTA, C_P, C_DUMP, C_E8, C_QS, C_SLOT, C_TOK = 0, 128, 256, 384, 385, 386, 387, 389, 453
C_W = 461
NB_AHEAD = 4
SLOPE0 = 2.0 ** (-2.0 ** (3 - H.bit_length() + 1))


def decoder_kernel(nc, x, tok_ids, ctx_t, wqk, wv, wo, bqk, rows, gate_t, w13_t, w2_t, consts, bias, out):
    with ExitStack() as ctx:
        def sb(name, shape, dt=F32):
            return ctx.enter_context(nc.sbuf_tensor(name, shape, dt))

        def sem(name):
            return ctx.enter_context(nc.semaphore(name))

        rows_dram = nc.dram_tensor("rows_dram", (TOK, D), F32).ap()
        table_dram = [nc.dram_tensor(f"table_dram{i}", (E * CAP, 2), F32).ap() for i in range(CHAINS)]
        sums_dram = [nc.dram_tensor(f"sums_dram{i}", (TOK + P, D), F32).ap() for i in range(CHAINS)]

        X = sb("X", [P, NT, D])
        XB = sb("XB", [P, NT, D])
        TID = sb("TID", [P, NT], I32)
        CT = sb("CT", [P, KD, EX * CTX])
        CS = sb("CS", [P, 2, KD, EX * CTX], F32R)
        XS = sb("XS", [P, 2, 2, KD, S], F32R)
        WQK = sb("WQK", [P, KD, 2, D])
        WV = sb("WV", [P, KD, D])
        WO = sb("WO", [P, KD, D])
        BQK = sb("BQK", [P, 2, NG])
        BQN = sb("BQN", [P, PAIR, NG])
        BROW = sb("BROW", [P, 2, D])
        GT = sb("GT", [P, KD, E])
        C = sb("C", [P, C_W])
        NB = sb("NB", [P, H, SC])
        BIAS = sb("BIAS", [P, 2, SC])
        ZERO = sb("ZERO", [P, (TOK + P) * D // P])
        NEGH = sb("NEGH", [P, TB])
        TRI = sb("TRI", [P, P], BF16)
        ONES = sb("ONES", [P, P], BF16)
        ONEF = sb("ONEF", [P, P])
        GE = sb("GE", [P, 3, NT])
        MSK = sb("MSK", [P, NT, EX])

        ST = sb("ST", [P, 3, TB, 6])
        MV = sb("MV", [P, 3, TB, 2])
        VE = sb("VE", [P, 3, TB])
        RSTD = sb("RSTD", [P, 3, TB])
        XN = sb("XN", [P, 3, TB, D])
        XT = sb("XT", [P, len(ROWS), KD, S])
        QT = sb("QT", [P, 2, PAIR, NG, S])
        KT = sb("KT", [P, 2, NG, S])
        VA = sb("VA", [P, 2, TB, H, SLOT])
        MN = sb("MN", [P, 4, 2])
        PR = sb("PR", [P, 2, SC])
        PT = sb("PT", [P, 2, SC])
        OT = sb("OT", [P, 2, S])
        RS = sb("RS", [P, TB, H])
        AO = sb("AO", [P, TB, H, HD])
        X2 = sb("X2", [P, TB, D])
        Z = sb("Z", [P, TB, CTX])
        TH = sb("TH", [P, TB, CTX])
        AA = sb("AA", [P, TB, CTX])
        X3 = sb("X3", [P, NT, D])
        ML = sb("ML", [P, TB, 8])
        NM = sb("NM", [P, TB])
        EL = sb("EL", [P, TB, E])
        SE = sb("SE", [P, TB])
        RE = sb("RE", [P, TB])
        PB = sb("PB", [P, TB, E])
        M8 = sb("M8", [P, TB, 8])
        PX = sb("PX", [P, TB, E])
        SEL = sb("SEL", [P, TB, E])
        SELB = sb("SELB", [P, TB, E], BF16)
        CNT = sb("CNT", [P, E], BF16)
        CW = sb("CW", [P, TB, E])
        SV = sb("SV", [P, TB, E])
        V8 = sb("V8", [P, TB, 8])
        IX = sb("IX", [P, TB, 8], I32)
        EQ = sb("EQ", [P, TB, 8, E])
        DT = sb("DT", [P, TB, 8, 2])

        TABLE = sb("TABLE", [P, CHAINS, P * 2])
        NI = sb("NI", [E, 4], I32)
        NBF = sb("NBF", [E, 1], BF16)
        SN = sb("SN", [E, 4])
        M1 = sb("M1", [E, P])
        M2 = sb("M2", [E, P])
        CB = sb("CB", [P, P])
        LATE = sb("LATE", [P, P])
        NTF = sb("NTF", [P, 1])
        TI = sb("TI", [P, 1], I32)
        TF = sb("TF", [P, 2])
        IW = sb("IW", [P, MAXT + CHAINS, 2])
        IA = sb("IA", [P, MAXT])
        EJ = sb("EJ", [1, 3, MAXT], I32)
        NQI = sb("NQI", [1, 4], I32)

        XR = sb("XR", [P, CHAINS, D])
        IG = sb("IG", [P, CHAINS], I32)
        IS = sb("IS", [P, CHAINS], I32)
        XRT = sb("XRT", [P, CHAINS, KD, P])
        W13 = sb("W13", [P, CHAINS, KD, 2 * F])
        W2 = sb("W2", [P, CHAINS, D])
        SG = sb("SG", [P, CHAINS, P])
        SPARE = sb("SPARE", [P, 1])
        HT = sb("HT", [P, CHAINS, P])
        OB = sb("OB", [P, CHAINS, D])

        ps = ctx.enter_context(nc.psum_tensor("ps", [P, 8, 512], F32))

        ident = C[:, C_ID:C_ID + P]
        iota = C[:, C_IOTA:C_IOTA + P]
        nb_flat = NB[:, :, :].rearrange("p h s -> p (h s)")
        sums = [nb_flat[:, 0:NT * D], nb_flat[:, NT * D:2 * NT * D], nb_flat[:, 2 * NT * D:3 * NT * D], ZERO[:, 0:NT * D]]

        s_lx, s_lq, s_lk, s_lwv, s_lwo, s_lct, s_lbias, s_lc, s_lr = (
            sem(f"s_l{i}") for i in ("x", "q", "k", "wv", "wo", "ct", "bias", "c", "r"))
        s_lx0, s_nb = sem("s_lx0"), sem("s_nb")
        s_zero, s_zt, s_zs = sem("s_zero"), sem("s_zt"), sem("s_zs")
        s_pool0, s_ge, s_xb = sem("s_pool0"), sem("s_ge"), sem("s_xb")
        s_st, s_mv, s_ve, s_rstd, s_xn = (sem(f"s_{i}") for i in ("st", "mv", "ve", "rstd", "xn"))
        s_tp, s_xt = sem("s_tp"), sem("s_xt")
        s_unit, s_used = [sem(f"s_unit{i}") for i in range(2)], [sem(f"s_used{i}") for i in range(2)]
        s_sc, s_tr, s_ex, s_pp, s_pt, s_pv = (sem(f"s_{i}") for i in ("sc", "tr", "ex", "pp", "pt", "pv"))
        s_ot, s_rs = sem("s_ot"), sem("s_rs")
        s_cs, s_xs = sem("s_cs"), sem("s_xs")
        s_z, s_th, s_ag, s_aa, s_y = (sem(f"s_{i}") for i in ("z", "th", "ag", "aa", "y"))
        s_ml, s_nm, s_re, s_pb, s_m8, s_px, s_sel, s_cnt, s_sv, s_v8, s_sf, s_eq, s_wt, s_ix, s_dt, s_cw = (
            sem(f"s_{i}") for i in ("ml", "nm", "re", "pb", "m8", "px", "sel", "cnt", "sv", "v8", "sf", "eq", "wt", "ix", "dt", "cw"))
        s_rd = sem("s_rd")
        s_tab = [sem(f"s_tab{i}") for i in range(CHAINS)]
        s_lt = [sem(f"s_lt{i}") for i in range(CHAINS)]
        s_cn, s_ni, s_stt, s_m, s_cb, s_ti, s_iw, s_plan = (sem(f"s_{i}") for i in ("cn", "ni", "stt", "m", "cb", "ti", "iw", "plan"))

        def sems(name):
            return [sem(f"{name}{i}") for i in range(CHAINS)]

        s_ig, s_xr, s_w, s_et, s_ext, s_gu, s_sg, s_h, s_o, s_ob, s_add = (
            sems(f"s_{i}") for i in ("ig", "xr", "w", "et", "ext", "gu", "sg", "h", "o", "ob", "add"))
        s_fl, s_fs, s_out = [sems(f"s_fl{n}_") for n in range(2)], sem("s_fs"), sem("s_out")

        def produced(eng, p, name):
            n = UNIT_NO[p, name]
            eng.wait_ge(s_unit[n % 2], n // 2 + 1)
            return 6 + n % 2, s_used[n % 2]

        def consumed(eng, p, name):
            n = UNIT_NO[p, name]
            eng.wait_ge(s_used[n % 2], n // 2 + 1)

        xv = x.rearrange("(n p) d -> p n d", p=P)
        block = ctx.enter_context(nc.Block())

        @block.sync
        def _(sp):
            sp.dma_start(X[:, 0:TB, :], xv[:, 0:TB, :]).then_inc(s_lx0, 16)
            sp.dma_start(C[:, :], consts).then_inc(s_lc, 16)
            sp.dma_start(BQK[:, :, :], bqk).then_inc(s_lc, 16)
            sp.dma_start(TID[:, :], tok_ids).then_inc(s_lc, 16)
            for a, loaded in enumerate((s_lq, s_lk)):
                sp.dma_start(WQK[:, :, a, :], wqk[:, a, :].rearrange("(k p) m -> p k m", p=P)).then_inc(loaded, 16)
            sp.dma_start(BIAS[:, :, :], bias).then_inc(s_lbias, 16)
            sp.dma_start(BROW[:, :, :], rows.partition_broadcast(P)).then_inc(s_lr, 16)
            sp.dma_start(WV[:, :, :], wv.rearrange("(k p) m -> p k m", p=P)).then_inc(s_lwv, 16)
            sp.dma_start(X[:, TB:NT, :], xv[:, TB:NT, :]).then_inc(s_lx, 16)
            sp.dma_start(WO[:, :, :], wo.rearrange("(k p) m -> p k m", p=P)).then_inc(s_lwo, 16)
            sp.dma_start(CT[:, :, :], ctx_t.rearrange("(k p) m -> p k m", p=P)).then_inc(s_lct, 16)
            sp.dma_start(GT[:, :, :], gate_t.rearrange("(k p) m -> p k m", p=P)).then_inc(s_lct, 16)
            sp.wait_ge(s_zero, 1)
            for i in range(CHAINS):
                sp.dma_start(table_dram[i].rearrange("(p r) c -> p (r c)", p=P), ZERO[:, 0:E * CAP * 2 // P]).then_inc(s_zt, 16)
                sp.dma_start(sums_dram[i].rearrange("(p r) d -> p (r d)", p=P), ZERO[:, :]).then_inc(s_zs, 16)
            for T in range(NT):
                p, t = divmod(T, TB)
                sp.wait_ge(s_xn, LN_NO[p, f"ln3_{t}"] + 1)
                sp.dma_start(rows_dram[T * P:(T + 1) * P, :], XN[:, 2, t, :]).then_inc(s_rd, 16)
            sp.wait_ge(s_plan, 1)
            quads = sp.value_load(NQI[0:1, 0:1], min_val=LEAST, max_val=MAXT // CHAINS)

            def load(q, i):
                e = sp.value_load(EJ[0:1, 0, bass.ds(q * CHAINS + i, 1)], min_val=0, max_val=E - 1)
                sp.dma_start(W13[:, i, :, :], w13_t[bass.ds(e, 1)].rearrange("e (k p) m -> p (e k) m", p=P)).then_inc(s_w[i], 16)
                sp.dma_start(W2[:, i, :], w2_t[bass.ds(e, 1)].rearrange("e p m -> p (e m)")).then_inc(s_w[i], 16)

            for i in range(CHAINS):
                load(0, i)
            with sp.Fori(1, quads) as q:
                for i in range(CHAINS):
                    sp.wait_ge(s_o[i], q)
                    load(q, i)
            half = NT // 2
            for n in range(2):
                for i in range(CHAINS):
                    if n == 0:
                        sp.wait_ge(s_add[i], quads * 16)
                    sp.dma_start(sums[i].rearrange("p (n d) -> p n d", d=D)[:, n * half:(n + 1) * half, :],
                                 sums_dram[i][n * half * P:(n + 1) * half * P, :].rearrange("(n p) d -> p n d", p=P)).then_inc(s_fl[n][i], 16)
            ov = out.rearrange("(n p) d -> p n d", p=P)
            for n in range(2):
                sp.wait_ge(s_fs, (n + 1) * CHAINS)
                sp.dma_start(ov[:, n * half:(n + 1) * half, :], X3[:, n * half:(n + 1) * half, :]).then_inc(s_out, 16)
            sp.wait_ge(s_out, 32)

        @block.gpsimd
        def _(pool):
            pool.memset(NEGH[:, :], -0.5).then_inc(s_pool0, 1)
            pool.wait_ge(s_lc, 48)
            for i in range(PAIR):
                pool.tensor_scalar(BQN[:, i, :], BQK[:, 0, :], C[:, C_QS + i:C_QS + i + 1], None, ALU.mult).then_inc(s_pool0, 1)

            def prepare(n):
                if n == SLOTS[0] + 3:
                    pool.memset(ZERO[:, :], 0.0).then_inc(s_zero, 1)
                if n == SLOTS[0] + 4:
                    pool.memset(VA[:, :, :, :, HD:HD + 1], 1.0).then_inc(s_pool0, 1)
                    pool.memset(VA[:, :, :, :, HD + 1:SLOT], 0.0).then_inc(s_pool0, 1)
                    pool.memset(CNT[:, :], 0.0).then_inc(s_pool0, 1)
                    pool.memset(XR[:, :, :], 0.0).then_inc(s_pool0, 1)
                    pool.memset(TABLE[:, :, :], 0.0).then_inc(s_pool0, 1)
                    pool.memset(ONES[:, :], 1.0).then_inc(s_pool0, 1)
                    pool.memset(ONEF[:, :], 1.0).then_inc(s_pool0, 1)
                    pool.tensor_copy(TRI[:, :], C[:, C_TRI:C_TRI + P]).then_inc(s_pool0, 1)
                if n == 2:
                    pool.wait_ge(s_lct, 32)
                    for k in range(KD):
                        pool.tensor_copy(CS[:, 0, k, :], CT[:, k, :]).then_inc(s_cs, 1)
                        pool.wait_ge(s_cs, 2 * k + 1)
                        pool.tensor_tensor(CS[:, 1, k, :], CT[:, k, :], CS[:, 0, k, :].bitcast(F32), ALU.subtract).then_inc(s_cs, 1)
                if n == 1:
                    pool.wait_ge(s_lx0, 16)
                    pool.wait_ge(s_lx, 16)
                    pool.wait_ge(s_lr, 16)
                    for t in range(NT):
                        pool.tensor_tensor(XB[:, t, :], X[:, t, :], BROW[:, 1, :], ALU.add).then_inc(s_xb, 1)

            for n in SLOTS:
                for p, name, t in steps(n):
                    if kind(name) in NORMS:
                        k, ln = LN_NO[p, name], NORMS.index(kind(name))
                        pool.wait_ge(s_mv, k + 1)
                        pool.tensor_scalar(VE[:, ln, t:t + 1], MV[:, ln, t, 1:2], EPS, None, ALU.add).then_inc(s_ve, 1)
                        pool.wait_ge(s_ve, k + 1)
                        pool.tensor_tensor(RSTD[:, ln, t:t + 1], VE[:, ln, t:t + 1], NEGH[:, 0:1], ALU.pow).then_inc(s_rstd, 1)
                prepare(n)
                for part in range(PARTS):
                    for p, name, t in steps(n - part):
                        if kind(name) == "scatter":
                            T = p * TB + t
                            if part == 0:
                                pool.wait_ge(s_ix, T + 1)
                                pool.wait_ge(s_dt, (T + 1) * 2)
                                pool.wait_ge(s_zt, 16 * CHAINS)
                            for k in range(part * TOPK // PARTS, (part + 1) * TOPK // PARTS):
                                i, m = k % CHAINS, (T * TOPK + k) // CHAINS
                                if m:
                                    pool.wait_ge(s_tab[i], m * 16)
                                pool.indirect_dma_start(out=table_dram[i], out_offset=bass.IndirectOffsetOnAxis(ap=IX[:, t, k:k + 1].bitcast(U32), axis=0),
                                                        in_=DT[:, t, k, :], in_offset=None).then_inc(s_tab[i], 16)

            pool.wait_ge(s_ti, 1)
            for i in range(CHAINS):
                pool.wait_ge(s_tab[i], 16 * NT * TOPK // CHAINS)
                pool.indirect_dma_start(out=TABLE[:, i, :], out_offset=None, in_=table_dram[i].rearrange("(r s) c -> r (s c)", s=P),
                                        in_offset=bass.IndirectOffsetOnAxis(ap=TI[:, 0:1].bitcast(U32), axis=0),
                                        bounds_check=COLS - 1, oob_is_err=False).then_inc(s_lt[i], 16)

            pool.wait_ge(s_plan, 1)
            quads = pool.value_load(NQI[0:1, 0:1], min_val=LEAST, max_val=MAXT // CHAINS)
            past, now, ahead = (pool.alloc_register(f"bodies_{i}") for i in ("past", "now", "ahead"))
            for register, value in ((past, 0), (now, 1), (ahead, 2)):
                pool.reg_mov(register, value)
            pool.wait_ge(s_rd, 16 * NT)
            pool.wait_ge(s_zs, 16 * CHAINS)

            def gather(i):
                pool.indirect_dma_start(out=XR[:, i, :], out_offset=None, in_=rows_dram,
                                        in_offset=bass.IndirectOffsetOnAxis(ap=IG[:, i:i + 1].bitcast(U32), axis=0),
                                        bounds_check=TOK - 1, oob_is_err=False).then_inc(s_xr[i], 16)

            def add(i):
                pool.indirect_dma_start(out=sums_dram[i], out_offset=bass.IndirectOffsetOnAxis(ap=IS[:, i:i + 1].bitcast(U32), axis=0),
                                        in_=OB[:, i, :], in_offset=None, compute_op=ALU.add).then_inc(s_add[i], 16)

            for i in range(CHAINS):
                pool.wait_ge(s_ig[i], 1)
                gather(i)
            for i in range(CHAINS):
                pool.wait_ge(s_ig[i], 2)
                pool.wait_ge(s_et[i], 1)
                gather(i)
                if i >= 2:
                    pool.wait_ge(s_ob[i - 2], 1)
                    add(i - 2)
            with pool.Fori(1, quads):
                for register in (past, now, ahead):
                    pool.reg_add(register, register, 1)
                for i in range(CHAINS):
                    pool.wait_ge(s_lc, 48)
                    pool.wait_ge(s_ig[i], ahead)
                    pool.wait_ge(s_et[i], now)
                    gather(i)
                    j = (i - 2) % CHAINS
                    pool.wait_ge(s_lc, 48)
                    pool.wait_ge(s_ob[j], now if i >= 2 else past)
                    add(j)
            for i in range(2, CHAINS):
                pool.wait_ge(s_lc, 48)
                pool.wait_ge(s_ob[i], quads)
                add(i)
            for i in range(CHAINS):
                pool.wait_ge(s_xr[i], quads * 16 + 16)

        @block.scalar
        def _(act):
            act.wait_ge(s_pool0, 3)

            for n in SLOTS:
                j = n - 4
                if 0 <= j < B * H and j % GO == GO - 1:
                    m = j // GO
                    act.wait_ge(s_pv, j + 1)
                    if m >= 2:
                        act.wait_ge(s_tp, TURN_NO[divmod(m - 2, H // GO)[0], f"to{(m - 2) % (H // GO)}"] + 1)
                    act.activation(OT[:, m % 2, :], ps[:, 4, 0:S], ACT.Copy).then_inc(s_ot, 1)
                j = n - 2
                if 0 <= j < B * H:
                    act.wait_ge(s_pp, j + 1)
                    if j >= 2:
                        act.wait_ge(s_pv, j - 1)
                    act.activation(PT[:, j % 2, :], ps[:, 2 + j % 2, 0:SC], ACT.Copy).then_inc(s_pt, 1)
                if 0 <= n < B * H:
                    act.wait_ge(s_tr, (n + 1) * 2)
                    if n >= 2:
                        act.wait_ge(s_pp, n - 1)
                    for c, (lo, hi) in enumerate(((0, P), (P, SC))):
                        act.activation(PR[:, n % 2, lo:hi], ps[:, n % 2, lo:hi], ACT.Exp, bias=MN[:, n % 4, c:c + 1], scale=-1.0).then_inc(s_ex, 1)
                for p, name, t in steps(n):
                    if name == "tx":
                        act.wait_ge(s_tp, TURN_NO[p, name] + 1)
                        act.activation(XT[:, 0, :, :], ps[:, 5, :].rearrange("p (k s) -> p k s", k=KD), ACT.Copy).then_inc(s_xt, 1)
                    elif kind(name) in SPLIT:
                        act.wait_ge(s_tp, TURN_NO[p, name] + 1)
                        act.activation(XS[:, SPLIT.index(kind(name)), 0, :, t * P:(t + 1) * P], ps[:, 5, 0:KD * P].rearrange("p (k s) -> p k s", k=KD),
                                       ACT.Copy).then_inc(s_xs, 1)
                    elif kind(name) in ROWS:
                        act.wait_ge(s_tp, TURN_NO[p, name] + 1)
                        act.activation(XT[:, ROWS.index(kind(name)), :, t * P:(t + 1) * P], ps[:, 5, 0:KD * P].rearrange("p (k s) -> p k s", k=KD),
                                       ACT.Copy).then_inc(s_xt, 1)
                    if name == "q":
                        bank, used = produced(act, p, name)
                        for i in range(PAIR):
                            for g in range(NG):
                                last = act.activation(QT[:, p % 2, i, g, :], ps[:, bank, g * S:(g + 1) * S], ACT.Identity,
                                                      bias=BQN[:, i, g:g + 1], scale=C[:, C_QS + i:C_QS + i + 1])
                        last.then_inc(used, 1)
                    if kind(name) == "zb":
                        consumed(act, p, name)
                        if p:
                            act.wait_ge(s_ag, (p - 1) * TB + t + 1)
                        act.activation(TH[:, t, :], Z[:, t, :], ACT.Tanh, scale=0.5).then_inc(s_th, 1)
                    if kind(name) == "top":
                        bank, used = produced(act, p, f"lg_{t}")
                        act.wait_ge(s_nm, p * TB + t + 1)
                        if p:
                            act.wait_ge(s_pb, (p - 1) * TB + t + 1)
                        act.activation(EL[:, t, :], ps[:, bank, 0:E], ACT.Exp, bias=NM[:, t:t + 1], accum_out=SE[:, t:t + 1]).then_inc(used, 1)

            act.activation(SPARE[:, :], ident[:, 0:1], ACT.Silu)
            act.wait_ge(s_plan, 1)
            act.wait_ge(s_iw, 4)
            quads = act.value_load(NQI[0:1, 0:1], min_val=LEAST, max_val=MAXT // CHAINS)

            def gate(q, i):
                act.wait_ge(s_gu[i], q + 1)
                act.activation(SG[:, i, :], ps[:, 2 + i % 2, 0:P], ACT.Silu).then_inc(s_sg[i], 1)

            def rows_weighted(q, i, first=False):
                act.wait_ge(s_o[i], q + 1)
                if not first:
                    act.wait_ge(s_add[i], q * 16)
                act.activation(IS[:, i:i + 1], IA[:, bass.ds(q * CHAINS + i, 1)], ACT.Copy)
                act.activation(OB[:, i, :], ps[:, 4 + i % 2, 0:D], ACT.Copy,
                               scale=IW[:, bass.ds(q * CHAINS + i, 1), 1]).then_inc(s_ob[i], 1)

            def body(q, first=False):
                for i in range(CHAINS):
                    gate(q, i)
                    if i:
                        rows_weighted(q, i - 1, first)
                rows_weighted(q, CHAINS - 1, first)

            body(0, first=True)
            with act.Fori(1, quads) as q:
                body(q)

        @block.tensor
        def _(pe):
            pe.wait_ge(s_lc, 48)

            def turn(p, name, t):
                if TURN_NO[p, name]:
                    pe.wait_ge(s_xt, TURN_NO[p, name])
                if name == "tx":
                    for t in range(TB):
                        pe.wait_ge(s_xn, LN_NO[p, f"ln1_{t}"] + 1)
                        for k in range(KD):
                            last = pe.transpose(ps[:, 5, k * S + t * P:k * S + (t + 1) * P], XN[:, 0, t, k * P:(k + 1) * P], ident)
                elif name in OUTS:
                    m = p * (H // GO) + int(name[2])
                    pe.wait_ge(s_ot, m + 1)
                    for t in range(TB):
                        last = pe.transpose(ps[:, 5, t * P:(t + 1) * P], OT[:, m % 2, t * P:(t + 1) * P], ident)
                else:
                    if kind(name) == "tao":
                        pe.wait_ge(s_xt, TURN_NO[p, f"to{H // GO - 1}"] + 1)
                        rows_of = lambda k: AO[:, t, k * HG:(k + 1) * HG, :].rearrange("p h d -> p (h d)")
                    elif kind(name) == "ta":
                        pe.wait_ge(s_aa, p * TB + t + 1)
                        rows_of = lambda k: AA[:, t, k * P:(k + 1) * P]
                    else:
                        n = int(kind(name)[2])
                        pe.wait_ge(s_xn, LN_NO[p, f"ln{n}_{t}"] + 1)
                        rows_of = lambda k: XN[:, n - 1, t, k * P:(k + 1) * P]
                    for k in range(KD):
                        last = pe.transpose(ps[:, 5, k * P:(k + 1) * P], rows_of(k), ident)
                last.then_inc(s_tp, 1)

            def unit(p, name, t):
                n, what = UNIT_NO[p, name], kind(name)
                bank = 6 + n % 2
                if n >= 2:
                    pe.wait_ge(s_used[n % 2], n // 2)
                source = {"q": "tx", "k": "tx", "v": "tx", "wo": "tao", "za": "tx2", "zb": "tx2", "ya": "ta", "yb": "ta", "lg": "tx3"}.get(what)
                if source:
                    pe.wait_ge(s_xt, TURN_NO[p, source if source == "tx" else f"{source}_{t}"] + 1)
                    xt = XT[:, ROWS.index(source), :, :]
                    if source in SPLIT:
                        xs = XS[:, SPLIT.index(source), :, :, t * P:(t + 1) * P]
                if what in ("q", "k"):
                    pe.wait_ge(s_lq if name == "q" else s_lk, 16)
                    for g in range(NG):
                        for k in range(KD):
                            last = pe.matmul(ps[:, bank, g * S:(g + 1) * S], WQK[:, k, "qk".index(name), g * P:(g + 1) * P],
                                             xt[:, k, :], start=(k == 0), stop=(k == KD - 1))
                elif what == "v":
                    pe.wait_ge(s_lwv, 16)
                    for t in range(TB):
                        for k in range(KD):
                            last = pe.matmul(ps[:, bank, t * D:(t + 1) * D], xt[:, k, t * P:(t + 1) * P], WV[:, k, :],
                                             start=(k == 0), stop=(k == KD - 1))
                elif what == "cum":
                    pe.wait_ge(s_pool0, 11)
                    pe.wait_ge(s_sel, p * TB + t + 1)
                    if p or t:
                        pe.wait_ge(s_cnt, p * TB + t)
                    pe.matmul(ps[:, bank, 0:E], TRI[:, :], SELB[:, t, :], start=True, stop=False)
                    last = pe.matmul(ps[:, bank, 0:E], ONES[:, :], CNT[:, :], start=False, stop=True)
                elif source in SPLIT:
                    pe.wait_ge(s_cs, 2 * KD)
                    cols = slice(0, 512) if what[1] == "a" else slice(512, 1024)
                    passes = [(k, i, j) for k in range(KD) for i, j in ((0, 0), (0, 1), (1, 0))]
                    for k, i, j in passes:
                        last = pe.matmul(ps[:, bank, :], xs[:, i, k, :], CS[:, j, k, cols], start=(k, i, j) == passes[0], stop=(k, i, j) == passes[-1])
                else:
                    loaded, needed, weights = {"wo": (s_lwo, 16, WO[:, :, :]), "lg": (s_lct, 32, GT[:, :, :])}[what]
                    pe.wait_ge(loaded, needed)
                    for k in range(KD):
                        last = pe.matmul(ps[:, bank, 0:weights.shape[-1]], xt[:, k, t * P:(t + 1) * P], weights[:, k, :],
                                         start=(k == 0), stop=(k == KD - 1))
                last.then_inc(s_unit[n % 2], 1)

            for n in SLOTS:
                if 0 <= n < B * H:
                    p, h = divmod(n, H)
                    if h == 0:
                        consumed(pe, p, "q")
                        consumed(pe, p, "k")
                    if n >= 2:
                        pe.wait_ge(s_ex, (n - 1) * 2)
                    g, lo = h // HG, h % HG // PAIR * SLOT
                    q, k = QT[lo:lo + SLOT, p % 2, h % PAIR, g, :], KT[lo:lo + SLOT, p % 2, g, :]
                    pe.matmul(ps[:, n % 2, 0:P], q[:, 0:P], k[:, 0:P], start=True, stop=True, tile_position=(lo, 0))
                    pe.matmul(ps[:, n % 2, P:SC], q[:, P:S], k[:, 0:S], start=True, stop=True, tile_position=(lo, 0)).then_inc(s_sc, 1)
                j = n - 2
                if 0 <= j < B * H:
                    pe.wait_ge(s_ex, (j + 1) * 2)
                    if j >= 2:
                        pe.wait_ge(s_pt, j - 1)
                    for c in range(3):
                        last = pe.transpose(ps[:, 2 + j % 2, c * P:(c + 1) * P], PR[:, j % 2, c * P:(c + 1) * P], ident)
                    last.then_inc(s_pp, 1)
                j = n - 3
                if 0 <= j < B * H:
                    p, h = divmod(j, H)
                    lo = h % GO * SLOT
                    if h == 0:
                        consumed(pe, p, "v")
                    if h % GO == 0 and j:
                        pe.wait_ge(s_ot, j // GO)
                    pe.wait_ge(s_pt, j + 1)
                    pe.matmul(ps[lo:lo + SLOT, 4, 0:S], VA[:, p % 2, 0, h, :], PT[:, j % 2, 0:S], start=True, stop=False, tile_position=(0, lo))
                    pe.matmul(ps[lo:lo + SLOT, 4, P:S], VA[:, p % 2, 1, h, :], PT[:, j % 2, S:SC], start=False, stop=True,
                              tile_position=(0, lo)).then_inc(s_pv, 1)
                for p, name, t in steps(n):
                    if kind(name) in TURNS:
                        turn(p, name, t)
                    if kind(name) in UNITS:
                        unit(p, name, t)

            pe.wait_ge(s_cnt, B * TB)
            pe.matmul(ps[0:E, 0, 0:1], CNT[:, :], ONES[:, 0:1], start=True, stop=True).then_inc(s_cn, 1)
            pe.wait_ge(s_ni, 3)
            pe.matmul(ps[0:E, 0, 1:2], TRI[0:E, 0:E], NBF[:, :], start=True, stop=True)
            pe.matmul(ps[:, 0, 2:3], ONES[0:E, :], NBF[:, :], start=True, stop=True).then_inc(s_cn, 1)
            pe.wait_ge(s_m, 3)
            pe.matmul(ps[:, 1, 0:P], ONEF[0:E, :], M1[:, :], start=True, stop=True)
            pe.matmul(ps[:, 1, P:P + 1], M1[:, :], ONEF[0:E, 0:1], start=True, stop=True).then_inc(s_cn, 1)
            for i in range(CHAINS):
                pe.wait_ge(s_lt[i], 16)
                for c in range(2):
                    last = pe.matmul(ps[:, 2 + c, 0:P], TABLE[:, i, :].rearrange("p (s c) -> p s c", c=2)[:, :, c],
                                     ident, start=(i == 0), stop=(i == CHAINS - 1))
            last.then_inc(s_cn, 1)

            pe.wait_ge(s_plan, 1)
            quads = pe.value_load(NQI[0:1, 0:1], min_val=LEAST, max_val=MAXT // CHAINS)

            def rows_turned(q, i):
                for k in range(KD):
                    last = pe.transpose(ps[:, i % 2, k * P:(k + 1) * P], XR[:, i, k * P:(k + 1) * P], ident)
                last.then_inc(s_et[i], 1)

            def up(q, i, first=False):
                pe.wait_ge(s_w[i], q * 32 + 32)
                pe.wait_ge(s_ext[i], q + 1)
                if i >= 2:
                    pe.wait_ge(s_h[i - 2], q + 1)
                elif not first:
                    pe.wait_ge(s_h[i + 2], q)
                for c in range(2):
                    for k in range(KD):
                        last = pe.matmul(ps[:, 2 + i % 2, c * P:(c + 1) * P], W13[:, i, k, c * F:(c + 1) * F], XRT[:, i, k, :],
                                         start=(k == 0), stop=(k == KD - 1))
                last.then_inc(s_gu[i], 1)

            def down(i):
                pe.matmul(ps[:, 4 + i % 2, 0:D], HT[:, i, :], W2[:, i, :], start=True, stop=True).then_inc(s_o[i], 1)

            def body(q, first=False):
                for i in range(CHAINS):
                    if i < CHAINS - 1:
                        pe.wait_ge(s_xr[i + 1], q * 16 + 16)
                    else:
                        pe.wait_ge(s_xr[0], q * 16 + 32)
                    if i:
                        pe.wait_ge(s_ext[i - 1], q + 1)
                    elif not first:
                        pe.wait_ge(s_ext[CHAINS - 1], q)
                    rows_turned(q, (i + 1) % CHAINS)
                    up(q, i, first)
                    if i:
                        pe.wait_ge(s_h[i - 1], q + 1)
                        if i == CHAINS - 1:
                            pe.wait_ge(s_ob[0], q + 1)
                        elif not first:
                            pe.wait_ge(s_ob[i + 1], q)
                        down(i - 1)
                    elif not first:
                        pe.wait_ge(s_h[CHAINS - 1], q)
                        pe.wait_ge(s_ob[1], q)
                        down(CHAINS - 1)

            pe.wait_ge(s_xr[0], 16)
            rows_turned(0, 0)
            body(0, first=True)
            with pe.Fori(1, quads) as q:
                body(q)
            pe.wait_ge(s_h[CHAINS - 1], quads)
            pe.wait_ge(s_ob[1], quads)
            down(CHAINS - 1)

        @block.vector
        def _(dve):
            def masks():
                for n in range(3):
                    dve.tensor_scalar(GE[:, n, :], TID[:, :], float(THIRD * (n + 1)), None, ALU.is_ge).then_inc(s_ge, 1)
                dve.wait_ge(s_ge, 3)
                dve.tensor_scalar(MSK[:, :, 0], GE[:, 0, :], -1.0, 1.0, ALU.mult, ALU.add).then_inc(s_ge, 1)
                dve.tensor_tensor(MSK[:, :, 1], GE[:, 0, :], GE[:, 1, :], ALU.subtract).then_inc(s_ge, 1)
                dve.tensor_tensor(MSK[:, :, 2], GE[:, 1, :], GE[:, 2, :], ALU.subtract).then_inc(s_ge, 1)
                dve.tensor_copy(MSK[:, :, 3], GE[:, 2, :]).then_inc(s_ge, 1)
                dve.wait_ge(s_ge, 7)

            def mask(T, e):
                return MSK[:, T, e:e + 1]

            def step(p, name, t):
                what, T = kind(name), p * TB + t
                rows_in = {"1": X[:, T, :], "2": X2[:, t, :], "3": X3[:, T, :]}.get(what[-1])
                if what in NORMS:
                    k, ln = LN_NO[p, name], NORMS.index(what)
                    if p:
                        dve.wait_ge(s_xn, LN_NO[p - 1, name] + 1)
                    if what == "ln1":
                        dve.wait_ge(s_lx if p else s_lx0, 16)
                    else:
                        consumed(dve, p, f"wo_{t}" if what == "ln2" else f"yb_{t}")
                    dve.bn_stats(ST[:, ln, t, :], rows_in).then_inc(s_st, 1)
                    dve.wait_ge(s_st, k + 1)
                    dve.bn_aggr(MV[:, ln, t, :], ST[:, ln, t, :]).then_inc(s_mv, 1)
                if what in ("n1", "n2", "n3"):
                    ln = int(what[1]) - 1
                    dve.wait_ge(s_rstd, LN_NO[p, f"ln{ln + 1}_{t}"] + 1)
                    if p:
                        dve.wait_ge(s_tp, TURN_NO[p - 1, ("tx", f"tx2_{t}", f"tx3_{t}")[ln]] + 1)
                        if ln == 2:
                            dve.wait_ge(s_rd, T * 16)
                    dve.tensor_scalar(XN[:, ln, t, :], rows_in, MV[:, ln, t, 0:1], RSTD[:, ln, t:t + 1], ALU.subtract, ALU.mult).then_inc(s_xn, 1)
                if what in OUTS:
                    h = int(what[2]) * GO
                    o = ps[:, 5, 0:S].rearrange("p (t h d) -> p t h d", t=TB, h=GO)
                    dve.wait_ge(s_tp, TURN_NO[p, name] + 1)
                    dve.reciprocal(RS[:, :, h:h + GO], o[:, :, :, HD]).then_inc(s_rs, 1)
                    dve.wait_ge(s_rs, p * (H // GO) + h // GO + 1)
                    if p:
                        dve.wait_ge(s_tp, TURN_NO[p - 1, f"tao_{TB - 1}"] + 1)
                    dve.tensor_tensor(AO[:, :, h:h + GO, :], o[:, :, :, 0:HD], RS[:, :, h:h + GO].unsqueeze(3).to_broadcast([P, TB, GO, HD]),
                                      ALU.mult).then_inc(s_xt, 1)
                if what in SPLIT:
                    xs = XS[:, SPLIT.index(what), :, :, t * P:(t + 1) * P]
                    dve.wait_ge(s_xs, XS_NO[p, name] + 1)
                    dve.tensor_tensor(xs[:, 1], ps[:, 5, 0:KD * P].rearrange("p (k s) -> p k s", k=KD), xs[:, 0].bitcast(F32),
                                      ALU.subtract).then_inc(s_xt, 1)
                if what == "k":
                    bank, used = produced(dve, p, name)
                    for g in range(NG):
                        last = dve.tensor_scalar(KT[:, p % 2, g, :], ps[:, bank, g * S:(g + 1) * S], BQK[:, 1, g:g + 1], None, ALU.add)
                    last.then_inc(used, 1)
                if what == "v":
                    bank, used = produced(dve, p, name)
                    dve.wait_ge(s_lr, 16)
                    dve.wait_ge(s_pool0, 11)
                    for t in range(TB):
                        last = dve.tensor_tensor(VA[:, p % 2, t, :, 0:HD], ps[:, bank, t * D:(t + 1) * D].rearrange("p (h d) -> p h d", h=H),
                                                 BROW[:, 0, :].rearrange("p (h d) -> p h d", h=H), ALU.add)
                    last.then_inc(used, 1)
                if what == "wo":
                    bank, used = produced(dve, p, name)
                    dve.wait_ge(s_xb, NT)
                    dve.tensor_tensor(X2[:, t, :], ps[:, bank, 0:D], XB[:, T, :], ALU.add).then_inc(used, 1)
                if what in ("za", "zb"):
                    bank, used = produced(dve, p, name)
                    half = "ab".index(what[1])
                    if half == 0:
                        if p:
                            dve.wait_ge(s_aa, (p - 1) * TB + t + 1)
                        dve.tensor_scalar(Z[:, t, :], ps[:, bank, 0:D], mask(T, 0), None, ALU.mult).then_inc(s_z, 1)
                    else:
                        consumed(dve, p, f"za_{t}")
                        dve.scalar_tensor_tensor(Z[:, t, :], ps[:, bank, 0:D], mask(T, 2), Z[:, t, :], ALU.mult, ALU.add).then_inc(s_z, 1)
                    dve.wait_ge(s_z, T * 2 + half + 1)
                    dve.scalar_tensor_tensor(Z[:, t, :], ps[:, bank, D:2 * D], mask(T, half * 2 + 1), Z[:, t, :], ALU.mult, ALU.add).then_inc(used, 1)
                if what == "a":
                    dve.wait_ge(s_th, T + 1)
                    if p:
                        dve.wait_ge(s_tp, TURN_NO[p - 1, f"ta_{t}"] + 1)
                    dve.scalar_tensor_tensor(AA[:, t, :], TH[:, t, :], 1.0, Z[:, t, :], ALU.add, ALU.mult).then_inc(s_ag, 1)
                    dve.wait_ge(s_ag, T + 1)
                    dve.scalar_tensor_tensor(AA[:, t, :], AA[:, t, :], 0.5, Z[:, t, :], ALU.mult, ALU.mult).then_inc(s_aa, 1)
                if what in ("ya", "yb"):
                    bank, used = produced(dve, p, name)
                    half = "ab".index(what[1])
                    x3 = X3[:, T, :]
                    if half:
                        consumed(dve, p, f"ya_{t}")
                    dve.scalar_tensor_tensor(x3, ps[:, bank, 0:D], mask(T, half * 2), x3 if half else X2[:, t, :], ALU.mult, ALU.add).then_inc(s_y, 1)
                    dve.wait_ge(s_y, T * 2 + half + 1)
                    dve.scalar_tensor_tensor(x3, ps[:, bank, D:2 * D], mask(T, half * 2 + 1), x3, ALU.mult, ALU.add).then_inc(used, 1)
                if what == "top":
                    bank, used = produced(dve, p, f"lg_{t}")
                    dve.max(ML[:, t, :], ps[:, bank, 0:E]).then_inc(s_ml, 1)
                    dve.wait_ge(s_ml, T + 1)
                    dve.tensor_scalar(NM[:, t:t + 1], ML[:, t, 0:1], -1.0, None, ALU.mult).then_inc(s_nm, 1)
                if what == "pick":
                    consumed(dve, p, f"lg_{t}")
                    dve.reciprocal(RE[:, t:t + 1], SE[:, t:t + 1]).then_inc(s_re, 1)
                    dve.wait_ge(s_re, T + 1)
                    dve.tensor_scalar(PB[:, t, :], EL[:, t, :], RE[:, t:t + 1], None, ALU.mult).then_inc(s_pb, 1)
                    dve.wait_ge(s_pb, T + 1)
                    dve.max(M8[:, t, :], PB[:, t, :]).then_inc(s_m8, 1)
                    dve.wait_ge(s_m8, T + 1)
                    dve.match_replace(PX[:, t, :], M8[:, t, :], PB[:, t, :], -1.0).then_inc(s_px, 1)
                    dve.wait_ge(s_px, T + 1)
                    dve.tensor_scalar(SELB[:, t, :], PX[:, t, :], 0.0, None, ALU.is_lt).then_inc(s_sel, 1)
                    dve.tensor_scalar(SEL[:, t, :], PX[:, t, :], 0.0, None, ALU.is_lt).then_inc(s_sf, 1)
                    dve.wait_ge(s_sf, T + 1)
                    dve.tensor_tensor(CW[:, t, :], PB[:, t, :], SEL[:, t, :], ALU.mult).then_inc(s_cw, 1)
                if what == "slot":
                    bank, used = produced(dve, p, f"cum_{t}")
                    if T:
                        dve.wait_ge(s_cnt, T)
                    dve.tensor_tensor(CNT[:, :], CNT[:, :], SELB[:, t, :], ALU.add).then_inc(s_cnt, 1)
                    dve.tensor_tensor(SV[:, t, :], ps[:, bank, 0:E], C[:, C_SLOT:C_SLOT + E], ALU.add).then_inc(used, 1)
                    consumed(dve, p, f"cum_{t}")
                    dve.tensor_tensor(SV[:, t, :], SV[:, t, :], SEL[:, t, :], ALU.mult).then_inc(s_sv, 1)
                    dve.wait_ge(s_sv, T + 1)
                    dve.max(V8[:, t, :], SV[:, t, :]).then_inc(s_v8, 1)
                    dve.wait_ge(s_v8, T + 1)
                    if p:
                        for i in range(CHAINS):
                            dve.wait_ge(s_tab[i], (T - 1) * 2 * 16)
                    dve.tensor_scalar(IX[:, t, :], V8[:, t, :], -1.0, None, ALU.add).then_inc(s_ix, 1)
                if what == "same":
                    dve.tensor_tensor(EQ[:, t, :, :], V8[:, t, :].unsqueeze(2).to_broadcast([P, TOPK, E]),
                                      SV[:, t, :].unsqueeze(1).to_broadcast([P, TOPK, E]), ALU.is_equal).then_inc(s_eq, 1)
                if what == "weigh":
                    dve.wait_ge(s_eq, T + 1)
                    dve.wait_ge(s_cw, T + 1)
                    dve.tensor_tensor(EQ[:, t, :, :], EQ[:, t, :, :], CW[:, t, :].unsqueeze(1).to_broadcast([P, TOPK, E]), ALU.mult).then_inc(s_wt, 1)
                if what == "pairs":
                    dve.tensor_copy(DT[:, t, :, 0], C[:, C_TOK + T:C_TOK + T + 1].to_broadcast([P, TOPK])).then_inc(s_dt, 1)
                    dve.wait_ge(s_wt, T + 1)
                    dve.tensor_reduce(DT[:, t, :, 1], EQ[:, t, :, :], AX_X, ALU.add).then_inc(s_dt, 1)

            for n in SLOTS:
                if n == AT["q"] + 1:
                    dve.wait_ge(s_lc, 48)
                    masks()
                if 0 <= n + NB_AHEAD < H:
                    h = n + NB_AHEAD
                    dve.wait_ge(s_lbias, 16)
                    dve.scalar_tensor_tensor(NB[:, h, :], BIAS[:, 0, :], SLOPE0 ** (h + 1), BIAS[:, 1, :], ALU.mult, ALU.add).then_inc(s_nb, 1)
                if 0 <= n < H:
                    dve.wait_ge(s_nb, n + 1)
                if 0 <= n < B * H:
                    dve.wait_ge(s_sc, n + 1)
                    for c, (lo, hi) in enumerate(((0, P), (P, SC))):
                        dve.tensor_tensor_reduce(ps[:, n % 2, lo:hi], ps[:, n % 2, lo:hi], NB[:, n % H, lo:hi], 1.0, 3e38, ALU.add, ALU.min,
                                                 MN[:, n % 4, c:c + 1]).then_inc(s_tr, 1)
                for p, name, t in steps(n):
                    step(p, name, t)

            dve.wait_ge(s_cn, 1)
            dve.tensor_scalar(NI[:, 0:1], ps[0:E, 0, 0:1], float(P - 1), None, ALU.add).then_inc(s_ni, 1)
            dve.wait_ge(s_ni, 1)
            dve.tensor_scalar(NI[:, 1:2], NI[:, 0:1], 7, None, ALU.logical_shift_right).then_inc(s_ni, 1)
            dve.wait_ge(s_ni, 2)
            dve.tensor_copy(NBF[:, :], NI[:, 1:2]).then_inc(s_ni, 1)
            dve.wait_ge(s_cn, 2)
            dve.tensor_copy(SN[:, 0:1], ps[0:E, 0, 1:2]).then_inc(s_stt, 1)
            dve.tensor_copy(NTF[:, :], ps[:, 0, 2:3]).then_inc(s_stt, 1)
            dve.wait_ge(s_ni, 3)
            dve.tensor_tensor(SN[:, 1:2], ps[0:E, 0, 1:2], NBF[:, :], ALU.add).then_inc(s_stt, 1)
            dve.tensor_tensor(SN[:, 2:3], C[0:E, C_E8:C_E8 + 1], ps[0:E, 0, 1:2], ALU.subtract).then_inc(s_stt, 1)
            dve.wait_ge(s_stt, 4)
            dve.tensor_scalar(M1[:, :], C[0:E, C_IOTA:C_IOTA + P], SN[:, 2:3], None, ALU.add).then_inc(s_m, 1)
            dve.wait_ge(s_m, 1)
            dve.scalar_tensor_tensor(M2[:, :], C[0:E, C_IOTA:C_IOTA + P], SN[:, 0:1], M1[:, :], ALU.is_ge, ALU.mult).then_inc(s_m, 1)
            dve.wait_ge(s_m, 2)
            dve.scalar_tensor_tensor(M1[:, :], C[0:E, C_IOTA:C_IOTA + P], SN[:, 1:2], M2[:, :], ALU.is_lt, ALU.mult).then_inc(s_m, 1)
            dve.tensor_scalar(LATE[:, :], iota, NTF[:, 0:1], 8.0 * TOK, ALU.is_ge, ALU.mult).then_inc(s_cb, 1)
            dve.tensor_scalar(NQI[0:1, 1:2], NTF[0:1, :], float(CHAINS - 1), None, ALU.add).then_inc(s_cb, 1)
            dve.wait_ge(s_cn, 3)
            dve.tensor_scalar(TF[:, 0:1], C[:, C_P:C_P + 1], NTF[:, 0:1], 8.0 * TOK, ALU.is_ge, ALU.mult).then_inc(s_cb, 1)
            dve.wait_ge(s_cb, 3)
            dve.tensor_tensor(TI[:, :], TF[:, 0:1], ps[:, 1, P:P + 1], ALU.add).then_inc(s_ti, 1)
            dve.tensor_tensor(CB[:, :], LATE[:, :], ps[:, 1, 0:P], ALU.add).then_inc(s_cb, 1)
            dve.tensor_scalar(NQI[0:1, 0:1], NQI[0:1, 1:2], 2, None, ALU.logical_shift_right).then_inc(s_cb, 1)
            dve.wait_ge(s_cb, 5)
            dve.tensor_scalar(EJ[:, 1, :], CB[0:1, :], 8.0 * E - 1, None, ALU.min).then_inc(s_cb, 1)
            dve.wait_ge(s_cb, 6)
            dve.tensor_scalar(EJ[:, 0, :], EJ[:, 1, :], 3, None, ALU.logical_shift_right).then_inc(s_cb, 1)
            dve.memset(IW[:, MAXT:MAXT + CHAINS, :], float(EMPTY)).then_inc(s_iw, 1)
            dve.wait_ge(s_cb, 7)
            dve.engine_nop().then_inc(s_plan, 1)
            dve.wait_ge(s_cn, 4)
            dve.tensor_scalar(IW[:, 0:MAXT, 0], ps[:, 2, 0:P], float(EMPTY), None, ALU.add).then_inc(s_iw, 1)
            dve.wait_ge(s_iw, 2)
            for i in range(CHAINS):
                dve.tensor_copy(IG[:, i:i + 1], IW[:, i, 0:1]).then_inc(s_ig[i], 1)
            dve.tensor_copy(IW[:, 0:MAXT, 1], ps[:, 3, 0:P]).then_inc(s_iw, 1)
            dve.tensor_scalar(IA[:, :], ps[:, 2, 0:P], float(EMPTY), C[:, C_DUMP:C_DUMP + 1], ALU.add, ALU.min).then_inc(s_iw, 1)

            quads = dve.value_load(NQI[0:1, 0:1], min_val=LEAST, max_val=MAXT // CHAINS)

            def rows_out(q, i):
                dve.wait_ge(s_et[i], q + 1)
                dve.tensor_copy(XRT[:, i, :, :], ps[:, i % 2, 0:KD * P].rearrange("p (k s) -> p k s", k=KD)).then_inc(s_ext[i], 1)

            def body(q):
                for i in range(CHAINS):
                    rows_out(q if i < CHAINS - 1 else q + 1, (i + 1) % CHAINS)
                    dve.wait_ge(s_xr[i], q * 16 + 16)
                    dve.tensor_copy(IG[:, i:i + 1], IW[:, bass.ds(q * CHAINS + CHAINS + i, 1), 0]).then_inc(s_ig[i], 1)
                    dve.wait_ge(s_sg[i], q + 1)
                    dve.tensor_tensor(HT[:, i, :], ps[:, 2 + i % 2, P:2 * P], SG[:, i, :], ALU.mult).then_inc(s_h[i], 1)

            rows_out(0, 0)
            body(0)
            with dve.Fori(1, quads) as q:
                body(q)

            half = NT // 2 * D
            for n in range(2):
                x3 = X3[:, n * NT // 2:(n + 1) * NT // 2, :].rearrange("p n d -> p (n d)")
                for i in range(CHAINS):
                    dve.wait_ge(s_fl[n][i], 16)
                    if i:
                        dve.wait_ge(s_fs, n * CHAINS + i)
                    dve.tensor_tensor(x3, x3, sums[i][:, n * half:(n + 1) * half], ALU.add).then_inc(s_fs, 1)


def _consts():
    import numpy as np

    c = np.zeros((P, C_W), np.float32)
    p, j = np.arange(P)[:, None], np.arange(P)[None, :]
    c[:, C_ID:C_ID + P] = p == j
    c[:, C_TRI:C_TRI + P] = p < j
    c[:, C_IOTA:C_IOTA + P] = j
    c[:, C_P] = np.arange(P)
    c[:, C_DUMP] = TOK + np.arange(P)
    c[:, C_SLOT:C_SLOT + E] = CAP * np.arange(E) + 1
    c[:, C_TOK:C_TOK + NT] = p + P * np.arange(NT) - EMPTY
    c[:, C_QS:C_QS + PAIR] = np.where(p // HD % PAIR == np.arange(PAIR), -(HD ** -0.5), 0)
    c[:, C_E8] = CAP // P * np.arange(P)
    key = np.concatenate([np.arange(P), np.arange(S)])
    query = np.arange(P)[:, None] + np.where(np.arange(SC) < P, 0, P)
    bias = np.zeros((P, 2, SC), np.float32)
    bias[:, 0] = S - 1 - key
    bias[:, 1] = np.where(key[None, :] > query, np.float32(1e37), np.float32(0))
    return c, bias


def kernel(x, itok_BxS_13_99985, ctx_2048, L0_attn_Wq, L0_attn_bq, L0_attn_Wk, L0_attn_bk, L0_attn_Wv, L0_attn_bv,
           L0_attn_Wo, L0_attn_bo, L0_ffn_gate_w, L0_ffn_w13, L0_ffn_w2):
    import numpy as np
    import concourse.bacc as bacc
    from concourse.bass_utils import run_bass_kernel_spmd

    consts, bias = _consts()
    arrays = {
        "x": np.asarray(x).reshape(TOK, D),
        "tok_ids": np.asarray(itok_BxS_13_99985).reshape(NT, P).T,
        "ctx_t": np.asarray(ctx_2048).transpose(2, 0, 1).reshape(D, EX * CTX),
        "wqk": np.stack([np.asarray(L0_attn_Wq), np.asarray(L0_attn_Wk)], axis=1),
        "wv": np.asarray(L0_attn_Wv),
        "wo": np.asarray(L0_attn_Wo),
        "bqk": np.stack([np.asarray(v).reshape(NG, P).T for v in (L0_attn_bq, L0_attn_bk)], axis=1),
        "rows": np.stack([np.asarray(L0_attn_bv), np.asarray(L0_attn_bo)]),
        "gate_t": np.asarray(L0_ffn_gate_w).T,
        "w13_t": np.asarray(L0_ffn_w13).transpose(0, 2, 1),
        "w2_t": np.asarray(L0_ffn_w2).transpose(0, 2, 1),
        "consts": consts,
        "bias": bias,
    }
    arrays = {k: np.ascontiguousarray(v) for k, v in arrays.items()}
    nc = bacc.Bacc("TRN2", target_bir_lowering=False, num_devices=1)
    args = [nc.dram_tensor(f"in_{k}", v.shape, mybir.dt.from_np(v.dtype), kind="ExternalInput").ap() for k, v in arrays.items()]
    out = nc.dram_tensor("out", (TOK, D), F32, kind="ExternalOutput").ap()
    decoder_kernel(nc, *args, out)
    r = run_bass_kernel_spmd(nc, [{f"in_{k}": v for k, v in arrays.items()}], core_ids=[0])
    return r.results[0]["out"].reshape(B, S, D)
```
